# Optimizing a Trainium2 kernel written in Bass

```python
import numpy as np
import jax
import jax.numpy as jnp

def _softmax(x, axis=-1):
    return jax.nn.softmax(x, axis=axis)

def _gelu(x):
    return jax.nn.gelu(x, approximate=True)

def _silu(x):
    return jax.nn.silu(x)

def _sigmoid(x):
    return jax.nn.sigmoid(x)

def _layernorm(x, axis=-1, eps=1e-05):
    m = jnp.mean(x, axis=axis, keepdims=True)
    v = jnp.var(x, axis=axis, keepdims=True)
    return (x - m) / jnp.sqrt(v + eps)

def _scatter_add(tgt, idx, src, axis=0):
    return tgt.at[idx].add(src)

def _segment_sum(src, seg, n):
    return jax.ops.segment_sum(src, seg, n)
kernel_name = 'mk_gnn_resnorm_d2_gnn_r32_5a5948'

def setup_inputs(seed: int=0):
    np.random.seed(seed)
    _w = jnp.asarray

    def _rec_inputs():
        import jax
        import jax.numpy as jnp
        _gk = jax.random.key(seed)
        x = -0.0009044 + 1 * jax.random.normal(jax.random.fold_in(_gk, 1), (3125, 32), jnp.float32)
        _s = jax.random.randint(jax.random.fold_in(_gk, 2), (50000,), 0, 3125, jnp.int32)
        _d = jax.random.randint(jax.random.fold_in(_gk, 3), (50000,), 0, 3125, jnp.int32)
        _loop = jnp.arange(3125, dtype=jnp.int32)
        src = jnp.concatenate([_s, _d, _loop])
        dst = jnp.concatenate([_d, _s, _loop])
        _o = jnp.argsort(dst, stable=True)
        src = src[_o]
        dst = dst[_o]
        edge_attr_16 = 0.000254156 + 0.999948 * jax.random.normal(jax.random.fold_in(_gk, 12), (103125, 16), jnp.float32)
        return (x, src, dst, edge_attr_16)
    x, src, dst, edge_attr_16 = _rec_inputs()

    def _L0_gnn_setup():
        import jax, jax.numpy as jnp
        import numpy as np
        N_NODES = 50000
        N_EDGES = 25000
        NODE_D, EDGE_D = (32, 16)
        FLOW_IN, FLOW_H, FLOW_OUT = (2 * NODE_D + EDGE_D, 64, 64)
        NODE_H, NODE_OUT = (64, 32)

        def _mlp(h, W1, b1, W2, b2):
            h = jax.nn.relu(h @ W1 + b1)
            return h @ W2 + b2
        key = jax.random.key(seed)
        ks = jax.random.split(key, 8)
        return {'x': jax.random.normal(ks[0], (N_NODES, NODE_D), dtype=jnp.float32), 'edge_index': jax.random.randint(ks[1], (2, N_EDGES), 0, N_NODES, dtype=jnp.int64), 'edge_attr': jax.random.normal(ks[2], (N_EDGES, EDGE_D), dtype=jnp.float32), 'Wf1': jax.random.normal(ks[3], (FLOW_IN, FLOW_H), dtype=jnp.float32) * (1.0 / np.sqrt(FLOW_IN)), 'bf1': jnp.zeros((FLOW_H,), dtype=jnp.float32), 'Wf2': jax.random.normal(ks[4], (FLOW_H, FLOW_OUT), dtype=jnp.float32) * (1.0 / np.sqrt(FLOW_H)), 'bf2': jnp.zeros((FLOW_OUT,), dtype=jnp.float32), 'Wn1': jax.random.normal(ks[5], (FLOW_OUT, NODE_H), dtype=jnp.float32) * (1.0 / np.sqrt(FLOW_OUT)), 'bn1': jnp.zeros((NODE_H,), dtype=jnp.float32), 'Wn2': jax.random.normal(ks[6], (NODE_H, NODE_OUT), dtype=jnp.float32) * (1.0 / np.sqrt(NODE_H)), 'bn2': jnp.zeros((NODE_OUT,), dtype=jnp.float32)}
    _L0_gnn_all = _L0_gnn_setup()
    _L0_gnn_in = {k: v for k, v in _L0_gnn_all.items() if k in ('Wf1', 'bf1', 'Wf2', 'bf2', 'Wn1', 'bn1', 'Wn2', 'bn2')}
    del _L0_gnn_all

    def _L1_gnn_setup():
        import jax, jax.numpy as jnp
        import numpy as np
        N = 3125
        E = 50000
        F_IN = 32
        F_OUT = 32
        key = jax.random.key(seed)
        k1, k2, k3, k4, k5 = jax.random.split(key, 5)
        x = jax.random.normal(k1, (N, F_IN), dtype=jnp.float32)
        edge_src = jax.random.randint(k2, (E,), 0, N, dtype=jnp.int32)
        edge_dst = jax.random.randint(k3, (E,), 0, N, dtype=jnp.int32)
        bound = 1.0 / np.sqrt(2 * F_IN)
        W = jax.random.uniform(k4, (2 * F_IN, F_OUT), minval=-bound, maxval=bound, dtype=jnp.float32)
        b = jax.random.uniform(k5, (F_OUT,), minval=-bound, maxval=bound, dtype=jnp.float32)
        return {'x': x, 'W': W, 'b': b, 'edge_src': edge_src, 'edge_dst': edge_dst}
    _L1_gnn_all = _L1_gnn_setup()
    _L1_gnn_in = {k: v for k, v in _L1_gnn_all.items() if k in ('W', 'b')}
    del _L1_gnn_all
    return {'x': x, 'src': src, 'dst': dst, 'edge_attr_16': edge_attr_16, 'L0_gnn_Wf1': _L0_gnn_in['Wf1'], 'L0_gnn_bf1': _L0_gnn_in['bf1'], 'L0_gnn_Wf2': _L0_gnn_in['Wf2'], 'L0_gnn_bf2': _L0_gnn_in['bf2'], 'L0_gnn_Wn1': _L0_gnn_in['Wn1'], 'L0_gnn_bn1': _L0_gnn_in['bn1'], 'L0_gnn_Wn2': _L0_gnn_in['Wn2'], 'L0_gnn_bn2': _L0_gnn_in['bn2'], 'L1_gnn_W': _L1_gnn_in['W'], 'L1_gnn_b': _L1_gnn_in['b']}

def reference(x, src, dst, edge_attr_16, L0_gnn_Wf1, L0_gnn_bf1, L0_gnn_Wf2, L0_gnn_bf2, L0_gnn_Wn1, L0_gnn_bn1, L0_gnn_Wn2, L0_gnn_bn2, L1_gnn_W, L1_gnn_b):
    import jax
    import jax.numpy as jnp

    def _L0_gnn_ref(x, edge_index, edge_attr, Wf1, bf1, Wf2, bf2, Wn1, bn1, Wn2, bn2):
        import jax, jax.numpy as jnp
        import numpy as np
        N_NODES = 50000
        N_EDGES = 25000
        NODE_D, EDGE_D = (32, 16)
        FLOW_IN, FLOW_H, FLOW_OUT = (2 * NODE_D + EDGE_D, 64, 64)
        NODE_H, NODE_OUT = (64, 32)

        def _mlp(h, W1, b1, W2, b2):
            h = jax.nn.relu(h @ W1 + b1)
            return h @ W2 + b2
        past, future = (edge_index[0], edge_index[1])
        x_p = x[past]
        x_f = x[future]
        flow_fwd = jnp.concatenate([x_f, x_p, edge_attr], axis=1)
        flow_bwd = jnp.concatenate([x_p, x_f, edge_attr], axis=1)
        flow_total_in = jnp.concatenate([flow_fwd, flow_bwd], axis=0)
        flow_processed = _mlp(flow_total_in, Wf1, bf1, Wf2, bf2)
        dest = jnp.concatenate([future, past], axis=0)
        flow_total = jax.ops.segment_sum(flow_processed, dest, num_segments=x.shape[0])
        return _mlp(flow_total, Wn1, bn1, Wn2, bn2)

    def _L1_gnn_ref(x, W, b, edge_src, edge_dst):
        import jax, jax.numpy as jnp
        import numpy as np
        N = 3125
        E = 50000
        F_IN = 32
        F_OUT = 32
        n = x.shape[0]
        msgs = x[edge_src]
        summed = jax.ops.segment_sum(msgs, edge_dst, num_segments=n)
        cnt = jax.ops.segment_sum(jnp.ones_like(edge_dst, dtype=x.dtype), edge_dst, num_segments=n)
        neigh_mean = summed / jnp.maximum(cnt, 1.0)[:, None]
        h = jnp.concatenate([x, neigh_mean], axis=1)
        return jax.nn.relu(h @ W + b)
    edge_index = jnp.stack([src, dst])
    x = _layernorm(x + _L0_gnn_ref(x, edge_index, edge_attr_16, L0_gnn_Wf1, L0_gnn_bf1, L0_gnn_Wf2, L0_gnn_bf2, L0_gnn_Wn1, L0_gnn_bn1, L0_gnn_Wn2, L0_gnn_bn2), axis=-1)
    x = _layernorm(x + _L1_gnn_ref(x, L1_gnn_W, L1_gnn_b, src, dst), axis=-1)
    return x

_drawn_inputs = setup_inputs


def setup_inputs(seed=0):
    import zlib

    import numpy as np

    out = dict(_drawn_inputs(seed))
    spreads = {'L0_gnn_bf1': (0.0, 0.1),
     'L0_gnn_bf2': (0.0, 0.1),
     'L0_gnn_bn1': (0.0, 2.0),
     'L0_gnn_bn2': (0.0, 2.0)}
    factors = {}
    for name, (base, spread) in spreads.items():
        noise = np.random.default_rng([zlib.crc32(name.encode()), seed]).standard_normal(out[name].shape)
        drawn = base * np.exp(spread * noise) if base else spread * noise
        out[name] = jnp.asarray(drawn.astype(out[name].dtype))
    for name, factor in factors.items():
        out[name] = (out[name] * factor).astype(out[name].dtype)
    return out
```

```python
import concourse.bass as bass
from concourse import mybir
from contextlib import ExitStack

P = 128
N, F = 3125, 32
E, FE = 103125, 16
HID = 64
NB = 26
NP = NB * P
PAD_NODE = N
TRASH = N + 1
G = 4
GS = 6
CS = G * GS
ES = CS * P
NS = -(-E // ES)
NG = NS * GS
EP = NS * ES
HW = HID + 1
SW = F + 1
R = 3
EPS = 1e-5
assert TRASH + P <= NP and N - 1 + P <= NP


def build(nc, x, src, dst, ea, Wf1, bf1, Wf2, bf2, Wn1, bn1, Wn2, bn2, W, b, out, force_general=False):
    fp32, i32, u32 = mybir.dt.float32, mybir.dt.int32, mybir.dt.uint32
    ALU, ACT, AX = mybir.AluOpType, mybir.ActivationFunctionType, mybir.AxisListType.X
    ds = bass.ds
    SRC, DST = 0, 1
    ctx = ExitStack()
    with ctx:
        def sb(name, shape, dt=fp32):
            return ctx.enter_context(nc.sbuf_tensor(name, shape, dt))

        def pb(name, shape):
            return ctx.enter_context(nc.psum_tensor(name, shape, fp32))

        def sem(name):
            return ctx.enter_context(nc.semaphore(name))

        ends_pad = [nc.dram_tensor(f"ends_pad{i}", (EP,), i32).ap() for i in range(2)]
        row_table = [nc.dram_tensor(f"row_table{i}", (NP, 2 * HID), fp32).ap() for i in range(2)]
        x1_table = nc.dram_tensor("x1_table", (NP, F), fp32).ap()
        hid_sum = [nc.dram_tensor(f"hid_sum{i}", (NP, HW), fp32).ap() for i in range(G)]
        nei_sum = [nc.dram_tensor(f"nei_sum{i}", (NP, SW), fp32).ap() for i in range(G)]

        xn = sb("xn", [P, NB, F])
        x1 = sb("x1", [P, NB, F])
        y = sb("y", [P, NB, F])
        centred = sb("centred", [P, NB, F])
        stat = sb("stat", [P, 4, NB])
        shared = sb("shared", [P, G * NB * HW])
        tables = shared[:, 0:NB * 4 * HID].rearrange("p (j f) -> p j f", j=NB)
        parts = shared[:, :].rearrange("p (t j f) -> p t j f", t=G, j=NB)
        hid_win_sum = sb("hid_win_sum", [HW, NP])
        nei_win_sum = sb("nei_win_sum", [SW, NP])
        Wends = sb("Wends", [F + 1, 4 * HID])
        Cblk = sb("Cblk", [G * FE, G, 2 * HID])
        Wf2b = sb("Wf2b", [HW, HID])
        Wn1s = sb("Wn1s", [HID, HID])
        bn1s = sb("bn1s", [HID, 1])
        Wn2b = sb("Wn2b", [HID + 1, F])
        Wb = sb("Wb", [2 * F + 1, F])
        eps = sb("eps", [P, 1])
        row_i = sb("row_i", [P, P], i32)
        col_i = sb("col_i", [P, 1], i32)
        row_no = sb("row_no", [P, P])
        col_no = sb("col_no", [P, 1])
        trash = sb("trash", [P, 1])
        below = sb("below", [P, P])
        ident = sb("ident", [P, P])
        ones = sb("ones", [P, 1])
        pads = sb("pads", [1, EP - E], i32)
        zrow = sb("zrow", [P, NB * HW])
        ends = [sb(f"ends{i}", [P, NS, CS], i32) for i in range(2)]
        base_i = sb("base_i", [P, NS], i32)
        base = sb("base", [P, NS])
        base_p = sb("base_p", [P, NS])
        local = sb("local", [P, NS, CS])
        reach = sb("reach", [P, 4])
        flag = sb("flag", [1, 1], i32)
        ends_bc = [sb(f"ends_bc{i}", [P, 2, ES], i32) for i in range(2)]
        ea_in = [sb(f"ea_in{r}", [P, G, FE]) for r in range(R)]
        win_rows = sb("win_rows", [P, 2, 2 * HID])
        get_idx = [[sb(f"get_idx{i}_{r}", [P, G], u32) for r in range(R)] for i in range(2)]
        put_idx = [[sb(f"put_idx{i}_{r}", [P, G], u32) for r in range(GS)] for i in range(2)]
        got = [sb(f"got{i}", [P, R, G, 2 * HID]) for i in range(2)]
        got1 = sb("nei_rows", [P, R, G, SW])
        same = [sb(f"same{i}", [P, R, G, P]) for i in range(2)]
        earlier = sb("earlier", [P, G, P])
        dup = sb("dup", [P, G])
        shift = sb("shift", [P, G])
        loc = sb("loc", [P, R, G])
        in_win = sb("in_win", [P, R, G, P])
        in_winT = sb("in_winT", [P, R, G, P])
        eaT = sb("eaT", [G * FE, 2, P])
        pre_sum = sb("pre_sum", [P, 2, G * 2 * HID])
        hid = sb("hid", [P, 2, G, 2 * HW])
        sums = [sb(f"sums{i}", [P, 2, G, HW]) for i in range(2)]
        nT = sb("nT", [2 * F + 1, 2 * P])
        fT = sb("fT", [HID, 2 * P])
        uT = sb("uT", [HID + 1, 2 * P])
        hT = sb("hT", [HW, 2 * P])
        cat = zrow[:, 0:NB * 2 * F].rearrange("p (j f) -> p j f", j=NB)

        ps_pre = [pb(f"ps_pre{i}", [P, 512]) for i in range(2)]
        ps_dd = [[pb(f"ps_dd{i}_{j}", [P, 512]) for j in range(2)] for i in range(2)]
        ps_eaT = pb("ps_eaT", [P, 512])
        ps_win = pb("ps_win", [P, 512])

        s_w = sem("weights_in")
        s_x = sem("x_in")
        s_pad = sem("padding_made")
        s_padded = sem("ends_padded")
        s_ends = sem("ends_in")
        s_iota = sem("iotas_made")
        s_zero = sem("zeros_made")
        s_const = sem("constants_made")
        s_chain = sem("vector_chain")
        s_xT = sem("xT_made")
        s_xTc = sem("xT_copied")
        s_rows = sem("rows_made")
        s_rowsc = sem("rows_copied")
        s_tab = sem("row_tables_written")
        s_far = sem("reach_counted")
        s_reach = sem("reach_made")
        s_flag = sem("flag_made")
        s_ea = [sem(f"ea_landed{r}") for r in range(R)]
        s_win_in = sem("win_rows_landed")
        s_bc = [sem(f"ends_bc_landed{i}") for i in range(2)]
        s_idx = sem("get_idx_ready")
        s_got = [[[sem(f"got{i}_{r}_{c}") for c in range(G)] for r in range(R)] for i in range(2)]
        s_link = sem("prep_chain")
        s_prep = sem("prep_ready")
        s_T = sem("eaT_made")
        s_Tc = sem("eaT_copied")
        s_pre = sem("pre_made")
        s_a = sem("add_chain")
        s_add = sem("pre_summed")
        s_hid = sem("hid_ready")
        s_B = sem("hid_used")
        s_sums = sem("sums_ready")
        s_sums_free = sem("sums_free")
        s_put = [sem(f"hid_scattered{c}") for c in range(G)]
        s_win_free = sem("ps_win_free")
        s_parts = sem("hid_sums_in")
        s_psum = sem("hid_summed")
        s_n = [sem(f"node_step{i}") for i in range(10)]
        s_ln = sem("layer_norm_chain")
        s_sq = sem("sqrt_asked")
        s_sqd = sem("sqrt_done")
        s_x1 = sem("x1_ready")
        s_x1t = sem("x1_table_written")
        s_idx1 = sem("l1_get_idx_ready")
        s_got1 = [[sem(f"l1_got_{r}_{c}") for c in range(G)] for r in range(R)]
        s_link1 = sem("l1_prep_chain")
        s_prep1 = sem("l1_prep_ready")
        s_B1 = sem("l1_rows_used")
        s_sums1 = sem("l1_sums_ready")
        s_sums1_free = sem("l1_sums_free")
        s_put1 = [sem(f"l1_scattered{c}") for c in range(G)]
        s_win1_free = sem("l1_ps_win_free")
        s_parts1 = sem("l1_sums_in")
        s_m = [sem(f"l1_node_step{i}") for i in range(10)]
        s_out = sem("out_written")

        NPAIR = NB // 2
        FULLX, RESTX = N // NB, N % NB
        ELAST = E - (NS - 1) * ES
        FULLE, RESTE = ELAST // CS, ELAST % CS
        W_DMAS = 4 + 4 + 2 * G + 2 + 1 + 1 + 2 + 2

        def bc_rows(side, s):
            return ends_pad[side][ds(s * ES, ES)].rearrange("(a n) -> a n", a=1).to_broadcast([P, ES])

        block = ctx.enter_context(nc.Block())

        @block.sync
        def _(sp):
            for side, e in ((SRC, src), (DST, dst)):
                sp.dma_start(ends_pad[side][0:E].rearrange("(a n) -> a n", a=75),
                             e.rearrange("(a n) -> a n", a=75)).then_inc(s_padded, 16)
            sp.wait_ge(s_pad, 1)
            for side in range(2):
                sp.dma_start(ends_pad[side][E:EP].rearrange("(a n) -> a n", a=1), pads[:, :]).then_inc(s_padded, 16)
            sp.wait_ge(s_zero, 1)
            sp.dma_start(xn[0:FULLX, :, :], x[0:FULLX * NB, :].rearrange("(p j) f -> p j f", j=NB)).then_inc(s_x, 16)
            sp.dma_start(xn[FULLX:FULLX + 1, 0:RESTX, :],
                         x[FULLX * NB:N, :].rearrange("(p j) f -> p j f", j=RESTX)).then_inc(s_x, 16)
            sp.wait_ge(s_padded, 64)
            for side in range(2):
                sp.dma_start(ends[side][:, :, :],
                             ends_pad[side].rearrange("(s p c) -> p s c", p=P, c=CS)).then_inc(s_ends, 16)
            with nc.allow_non_contiguous_dma(reason="one base per supertile"):
                sp.dma_start(base_i[:, :], ends_pad[DST].rearrange("(s e) -> e s", e=ES)[0:1, :]
                             .to_broadcast([P, NS])).then_inc(s_ends, 16)
            sp.wait_ge(s_rowsc, NPAIR + 1)
            for side in range(2):
                lo = 2 * HID * (1 - side)
                sp.dma_start(row_table[side].rearrange("(p j) f -> p j f", j=NB),
                             tables[:, :, lo:lo + 2 * HID]).then_inc(s_tab, 16)
            sp.wait_ge(s_flag, 1)
            fast = sp.value_load(flag[0:1, 0:1], min_val=0, max_val=1)

            def program(windows):
                if windows:
                    sp.wait_ge(s_tab, 32)

                def load_ea(n, s, g):
                    sp.wait_ge(s_T, n + 1)
                    cols = slice(g * G, (g + 1) * G)
                    if isinstance(s, int) and s == NS - 1:
                        first, rest = s * ES, min(G, RESTE - g * G)
                        sp.dma_start(ea_in[g % R][0:FULLE, :, :],
                                     ea[first:first + FULLE * CS, :].rearrange("(p c) f -> p c f", c=CS)[:, cols, :]).then_inc(s_ea[g % R], 16)
                        first += FULLE * CS + g * G
                        sp.dma_start(ea_in[g % R][FULLE:FULLE + 1, 0:rest, :],
                                     ea[first:first + rest, :].rearrange("(p c) f -> p c f", p=1)).then_inc(s_ea[g % R], 16)
                    else:
                        sp.dma_start(ea_in[g % R][:, :, :],
                                     ea[ds(s * ES, ES), :].rearrange("(p c) f -> p c f", c=CS)[:, cols, :]).then_inc(s_ea[g % R], 16)

                def load_supertile(s):
                    if windows:
                        first = sp.value_load(base_i[0:1, ds(s, 1)], min_val=0, max_val=N - 1)
                        sp.dma_start(win_rows[:, ds(s % 2, 1), :].rearrange("p a f -> p (a f)"),
                                     row_table[DST][ds(first, P), :]).then_inc(s_win_in, 16)
                    for side in range(2):
                        sp.dma_start(ends_bc[side][:, ds(s % 2, 1), :].rearrange("p a e -> p (a e)"),
                                     bc_rows(side, s)).then_inc(s_bc[side], 16)

                def supertile(s, first=False):
                    for g in range(GS):
                        load_ea(s * GS + g, s, g)
                        if g == R and not (isinstance(s, int) and s == NS - 1):
                            sp.wait_ge(s_pre, s * GS + 1)
                            sp.wait_ge(s_prep, s * GS + 1)
                            load_supertile(s + 1)

                load_supertile(0)
                with sp.Fori(0, NS - 1) as s:
                    supertile(s)
                supertile(NS - 1)
                puts = NG if windows else 2 * NG
                for t in range(G):
                    sp.wait_ge(s_put[t], 16 * (1 + puts))
                    sp.dma_start(parts[:, t, :, :], hid_sum[t].rearrange("(p j) f -> p j f", j=NB)).then_inc(s_parts, 16)
                sp.wait_ge(s_x1, 1)
                sp.dma_start(x1_table.rearrange("(p j) f -> p j f", j=NB), x1[:, :, :]).then_inc(s_x1t, 16)
                if not windows:
                    sp.wait_ge(s_prep, NG)
                    sp.dma_start(ends_bc[DST][:, 0, :], bc_rows(DST, 0)).then_inc(s_bc[DST], 16)
                    with sp.Fori(1, NS) as s:
                        sp.wait_ge(s_prep1, (s - 1) * GS + 1)
                        sp.dma_start(ends_bc[DST][:, s % 2, :], bc_rows(DST, s)).then_inc(s_bc[DST], 16)
                    for t in range(G):
                        sp.wait_ge(s_put1[t], 16 * (1 + NG))
                        sp.dma_start(parts[:, t, :, 0:SW], nei_sum[t].rearrange("(p j) f -> p j f", j=NB)).then_inc(s_parts1, 16)
                sp.wait_ge(s_x1t, 16)
                sp.wait_ge(s_m[9], 1)
                sp.dma_start(out[0:FULLX * NB, :].rearrange("(p j) f -> p j f", j=NB), y[0:FULLX, :, :]).then_inc(s_out, 16)
                sp.dma_start(out[FULLX * NB:N, :].rearrange("(p j) f -> p j f", j=RESTX),
                             y[FULLX:FULLX + 1, 0:RESTX, :]).then_inc(s_out, 16)
                sp.wait_ge(s_out, 32)

            with sp.If(fast == 1):
                program(True)
            with sp.Else():
                program(False)

        @block.gpsimd
        def _(pool):
            nc.gpsimd.iota(row_i[:, :], pattern=[[1, P]], base=0, channel_multiplier=0).then_inc(s_iota, 1)
            nc.gpsimd.iota(col_i[:, :], pattern=[[0, 1]], base=0, channel_multiplier=1).then_inc(s_iota, 1)
            nc.gpsimd.memset(got1[:, :, :, F:SW], 1.0).then_inc(s_iota, 1)
            pool.wait_ge(s_zero, 1)
            for t in range(G):
                pool.dma_start(hid_sum[t].rearrange("(p j) f -> p (j f)", p=P), zrow[:, :]).then_inc(s_put[t], 16)
            pool.wait_ge(s_tab, 32)
            for t in range(G):
                pool.wait_ge(s_put[t], 16)
            pool.wait_ge(s_flag, 1)
            fast = pool.value_load(flag[0:1, 0:1], min_val=0, max_val=1)

            def program(windows):
                sides = (SRC,) if windows else (SRC, DST)
                if not windows:
                    for t in range(G):
                        pool.dma_start(nei_sum[t].rearrange("(p j) f -> p (j f)", p=P), zrow[:, 0:NB * SW]).then_inc(s_put1[t], 16)
                    for t in range(G):
                        pool.wait_ge(s_put1[t], 16)

                def gather(n, g):
                    pool.wait_ge(s_idx, n + 1)
                    pool.nop(nofuse=True)
                    for side in sides:
                        for c in range(G):
                            pool.indirect_dma_start(
                                out=got[side][:, g % R, c, :], out_offset=None, in_=row_table[side],
                                in_offset=bass.IndirectOffsetOnAxis(ap=get_idx[side][g % R][:, c:c + 1], axis=0))\
                                .then_inc(s_got[side][g % R][c], 16)

                def scatter(n, g):
                    pool.wait_ge(s_sums, n + 1)
                    pool.wait_ge(s_prep, n + 1)
                    for c in range(G):
                        pool.wait_ge(s_put[c], 16 * (len(sides) * n + 1))
                    pool.nop(nofuse=True).then_inc(s_sums_free, 1)
                    for j, side in enumerate(sides):
                        for c in range(G):
                            if j:
                                pool.wait_ge(s_put[c], 16 * (len(sides) * n + 2))
                                pool.nop(nofuse=True)
                            pool.indirect_dma_start(
                                out=hid_sum[c], in_=sums[side][:, g % 2, c, :], in_offset=None,
                                out_offset=bass.IndirectOffsetOnAxis(ap=put_idx[side][g][:, c:c + 1], axis=0),
                                compute_op=ALU.add).then_inc(s_put[c], 16)

                pool.sem_inc(s_sums_free, 1)
                gather(0, 0)
                gather(1, 1)
                with pool.Fori(0, NS - 1) as s:
                    for g in range(GS):
                        gather(s * GS + g + 2, (g + 2) % GS)
                        scatter(s * GS + g, g)
                for g in range(GS):
                    n = NG - GS + g
                    if n + 2 < NG:
                        gather(n + 2, g + 2)
                    scatter(n, g)

                pool.wait_ge(s_x1t, 16)
                if not windows:
                    pool.sem_inc(s_sums1_free, 1)

                def gather1(n, g):
                    pool.wait_ge(s_idx1, n + 1)
                    pool.nop(nofuse=True)
                    for c in range(G):
                        pool.indirect_dma_start(
                            out=got1[:, g % R, c, 0:F], out_offset=None, in_=x1_table,
                            in_offset=bass.IndirectOffsetOnAxis(ap=get_idx[SRC][g % R][:, c:c + 1], axis=0))\
                            .then_inc(s_got1[g % R][c], 16)

                def scatter1(n, g):
                    pool.wait_ge(s_sums1, n + 1 + 2)
                    pool.wait_ge(s_prep1, n + 1)
                    for c in range(G):
                        pool.wait_ge(s_put1[c], 16 * (n + 1))
                    pool.nop(nofuse=True).then_inc(s_sums1_free, 1)
                    for c in range(G):
                        pool.indirect_dma_start(
                            out=nei_sum[c], in_=sums[DST][:, g % 2, c, 0:SW], in_offset=None,
                            out_offset=bass.IndirectOffsetOnAxis(ap=put_idx[DST][g][:, c:c + 1], axis=0),
                            compute_op=ALU.add).then_inc(s_put1[c], 16)

                gather1(0, 0)
                gather1(1, 1)
                with pool.Fori(0, NS - 1) as s:
                    for g in range(GS):
                        gather1(s * GS + g + 2, (g + 2) % GS)
                        if not windows:
                            scatter1(s * GS + g, g)
                for g in range(GS):
                    n = NG - GS + g
                    if n + 2 < NG:
                        gather1(n + 2, g + 2)
                    if not windows:
                        scatter1(n, g)

            with pool.If(fast == 1):
                program(True)
            with pool.Else():
                program(False)

        @block.scalar
        def _(act):
            act.wait_ge(s_zero, 1)
            for k in range(4):
                r = F * (k in (1, 2))
                act.dma_start(Wends[0:F, k * HID:(k + 1) * HID], Wf1[r:r + F, :]).then_inc(s_w, 16)
            for k in range(2):
                act.dma_start(Wends[F:F + 1, k * HID:(k + 1) * HID], bf1.rearrange("(a n) -> a n", a=1)).then_inc(s_w, 16)
                act.dma_start(Wends[F:F + 1, (2 + k) * HID:(3 + k) * HID], zrow[0:1, 0:HID]).then_inc(s_w, 16)
            for c in range(G):
                for k in range(2):
                    act.dma_start(Cblk[c * FE:(c + 1) * FE, c, k * HID:(k + 1) * HID], Wf1[2 * F:2 * F + FE, :]).then_inc(s_w, 16)
            act.dma_start(Wf2b[0:HID, :], Wf2).then_inc(s_w, 16)
            act.dma_start(Wf2b[HID:HW, :], bf2.rearrange("(a n) -> a n", a=1)).then_inc(s_w, 16)
            act.dma_start(Wn1s[:, :], Wn1).then_inc(s_w, 16)
            act.dma_start(bn1s[:, :], bn1.rearrange("(n a) -> n a", a=1)).then_inc(s_w, 16)
            act.dma_start(Wn2b[0:HID, :], Wn2).then_inc(s_w, 16)
            act.dma_start(Wn2b[HID:HID + 1, :], bn2.rearrange("(a n) -> a n", a=1)).then_inc(s_w, 16)
            act.dma_start(Wb[0:2 * F, :], W).then_inc(s_w, 16)
            act.dma_start(Wb[2 * F:2 * F + 1, :], b.rearrange("(a n) -> a n", a=1)).then_inc(s_w, 16)
            with act.Fori(0, NPAIR) as q:
                act.wait_ge(s_xT, q + 1)
                nc.scalar.activation(nT[0:F, :], ps_eaT[0:F, 0:2 * P], ACT.Copy).then_inc(s_xTc, 1)
            act.wait_ge(s_flag, 1)
            fast = act.value_load(flag[0:1, 0:1], min_val=0, max_val=1)

            def program(windows):
                sides = (SRC,) if windows else (SRC, DST)

                def copy_eaT(n, g):
                    act.wait_ge(s_T, R + n + 1)
                    nc.scalar.activation(eaT[:, g % 2, :], ps_eaT[0:G * FE, 0:P], ACT.Copy).then_inc(s_Tc, 1)

                def relu(n, g):
                    act.wait_ge(s_add, n + 1)
                    nc.scalar.activation(
                        hid[:, g % 2, :, :].rearrange("p c (k f) -> p c k f", k=2)[:, :, :, 0:HID],
                        pre_sum[:, g % 2, :].rearrange("p (c k f) -> p c k f", c=G, k=2), ACT.Relu).then_inc(s_hid, 1)

                def copy_sums(n, g):
                    act.wait_ge(s_B, R + n + 1)
                    act.wait_ge(s_sums_free, n + 1)
                    for side in sides:
                        last = nc.scalar.activation(
                            sums[side][:, g % 2, :, :],
                            ps_dd[side][g % 2][:, 0:G * HW].rearrange("p (c f) -> p c f", c=G), ACT.Copy)
                    last.then_inc(s_sums, 1)

                copy_eaT(0, 0)
                with act.Fori(0, NS - 1) as s:
                    for g in range(GS):
                        copy_eaT(s * GS + g + 1, (g + 1) % GS)
                        relu(s * GS + g, g)
                        copy_sums(s * GS + g, g)
                for g in range(GS):
                    n = NG - GS + g
                    if n + 1 < NG:
                        copy_eaT(n + 1, g + 1)
                    relu(n, g)
                    copy_sums(n, g)
                with act.Fori(0, NPAIR) as q:
                    act.wait_ge(s_n[2], q + 1)
                    nc.scalar.activation(fT[:, :], ps_pre[1][0:HID, 0:2 * P], ACT.Copy).then_inc(s_n[3], 1)
                    act.wait_ge(s_n[4], q + 1)
                    nc.scalar.activation(uT[0:HID, :], ps_dd[0][0][0:HID, 0:2 * P], ACT.Relu, bias=bn1s[:, 0:1]).then_inc(s_n[5], 1)
                act.wait_ge(s_sq, 1)
                nc.scalar.activation(stat[:, 2, :], stat[:, 1, :], ACT.Sqrt, bias=eps[:, 0:1], scale=1.0 / F).then_inc(s_sqd, 1)
                if not windows:
                    act.sem_inc(s_sums1, 2)

                    def copy_sums1(n, g):
                        act.wait_ge(s_B1, R + n + 1)
                        act.wait_ge(s_sums1_free, n + 1)
                        nc.scalar.activation(
                            sums[DST][:, g % 2, :, 0:SW],
                            ps_dd[DST][g % 2][:, 0:G * SW].rearrange("p (c f) -> p c f", c=G), ACT.Copy).then_inc(s_sums1, 1)
                    with act.Fori(0, NS) as s:
                        for g in range(GS):
                            copy_sums1(s * GS + g, g)
                with act.Fori(0, NPAIR) as q:
                    act.wait_ge(s_m[3], q + 1)
                    nc.scalar.activation(nT[0:2 * F, :], ps_pre[1][0:2 * F, 0:2 * P], ACT.Copy).then_inc(s_m[4], 1)
                    act.wait_ge(s_m[5], q + 1)
                    nc.scalar.activation(y[:, ds(2 * q, 2), :],
                                         ps_dd[0][0][:, 0:2 * F].rearrange("p (j f) -> p j f", j=2), ACT.Relu).then_inc(s_m[6], 1)
                act.wait_ge(s_sq, 2)
                nc.scalar.activation(stat[:, 2, :], stat[:, 1, :], ACT.Sqrt, bias=eps[:, 0:1], scale=1.0 / F).then_inc(s_sqd, 1)

            with act.If(fast == 1):
                program(True)
            with act.Else():
                program(False)

        @block.vector
        def _(dve):
            chain = [0]

            def link(ins):
                chain[0] += 1
                ins.then_inc(s_chain, 1)
                dve.wait_ge(s_chain, chain[0])

            v = nc.vector
            v.memset(pads[:, :], PAD_NODE).then_inc(s_pad, 1)
            v.memset(xn[:, :, :], 0.0)
            v.memset(Cblk[:, :, :], 0.0)
            v.memset(zrow[:, :], 0.0).then_inc(s_zero, 1)
            v.memset(nT[F:F + 1, :], 1.0)
            v.memset(nT[2 * F:2 * F + 1, :], 1.0)
            v.memset(uT[HID:HID + 1, :], 1.0)
            v.memset(ones[:, :], 1.0)
            v.memset(eps[:, :], EPS)
            for k in range(2):
                v.memset(hid[:, :, :, k * HW + HID:(k + 1) * HW], 1.0)
            v.memset(hid_win_sum[:, :], 0.0)
            v.memset(nei_win_sum[:, :], 0.0)
            dve.wait_ge(s_iota, 3)
            v.tensor_copy(row_no[:, :], row_i[:, :])
            link(v.tensor_copy(col_no[:, :], col_i[:, :]))
            v.tensor_scalar(trash[:, :], col_no[:, :], float(TRASH), None, ALU.add)
            v.tensor_scalar(below[:, :], row_no[:, :], col_no[:, 0:1], None, ALU.is_lt)
            v.tensor_scalar(ident[:, :], row_no[:, :], col_no[:, 0:1], None, ALU.is_equal).then_inc(s_const, 1)
            dve.sem_inc(s_rowsc, 1)
            with dve.Fori(0, NPAIR) as q:
                dve.wait_ge(s_rows, q + 1)
                v.tensor_copy(tables[:, ds(2 * q, 2), :], ps_pre[0][:, :].rearrange("p (j f) -> p j f", j=2)).then_inc(s_rowsc, 1)
            dve.wait_ge(s_ends, 48)
            link(v.tensor_copy(base[:, :], base_i[:, :]))
            v.tensor_scalar(base_p[:, :], base[:, :], col_no[:, 0:1], None, ALU.add)
            link(v.tensor_tensor(local[:, :, :], ends[DST][:, :, :],
                                 base[:, :].rearrange("p (s a) -> p s a", a=1).to_broadcast([P, NS, CS]), ALU.subtract))
            flat = local[:, :, :].rearrange("p s c -> p (s c)")
            v.tensor_reduce(out=reach[:, 0:1], in_=flat, axis=AX, op=ALU.max)
            link(v.tensor_reduce(out=reach[:, 1:2], in_=flat, axis=AX, op=ALU.min))
            v.tensor_scalar(reach[:, 2:3], reach[:, 0:1], P - 0.5, None, ALU.is_gt)
            link(v.tensor_scalar(reach[:, 1:2], reach[:, 1:2], -0.5, None, ALU.is_lt))
            v.tensor_tensor(reach[:, 3:4], reach[:, 1:2], reach[:, 2:3], ALU.add).then_inc(s_reach, 1)
            dve.wait_ge(s_far, 1)
            v.tensor_scalar(flag[:, :], ps_win[0:1, 0:1], -1.0 if force_general else 0.5, None, ALU.is_lt).then_inc(s_flag, 1)
            dve.wait_ge(s_flag, 1)
            fast = dve.value_load(flag[0:1, 0:1], min_val=0, max_val=1)

            def program(windows):
                sides = (SRC,) if windows else (SRC, DST)

                def copy_idx(s, g, which, signal):
                    for side in which:
                        last = v.tensor_copy(get_idx[side][g % R][:, :], col(side, s, g))
                    last.then_inc(signal, 1)

                def col(side, s, g):
                    return ends[side][:, ds(s, 1), g * G:(g + 1) * G].rearrange("p a c -> p (a c)")

                def bcast(side, s, g):
                    return ends_bc[side][:, ds(s % 2, 1), :].rearrange("p a (q c) -> p (a c) q", c=CS)[:, g * G:(g + 1) * G, :]

                def wide(small):
                    return small.rearrange("p (c a) -> p c a", a=1).to_broadcast([P, G, P])

                def rows(small):
                    return small.rearrange("p (a q) -> p a q", a=1).to_broadcast([P, G, P])

                def dedup(side, s, g, after):
                    after(v.tensor_tensor(same[side][:, g % R, :, :], bcast(side, s, g), wide(col(side, s, g)), ALU.is_equal))
                    after(v.tensor_tensor(earlier[:, :, :], same[side][:, g % R, :, :], rows(below[:, :]), ALU.mult))
                    v.tensor_scalar(shift[:, :], col(side, s, g), -1.0, trash[:, 0:1], ALU.mult, ALU.add)
                    after(v.tensor_reduce(out=dup[:, :], in_=earlier[:, :, :], axis=AX, op=ALU.max))
                    after(v.tensor_tensor(shift[:, :], shift[:, :], dup[:, :], ALU.mult))
                    return v.tensor_tensor(put_idx[side][g][:, :], shift[:, :], col(side, s, g), ALU.add)

                def in_window(s, g, after):
                    after(v.tensor_scalar(loc[:, g % R, :], col(DST, s, g), base[:, ds(s, 1)], None, ALU.subtract))
                    return v.tensor_tensor(in_win[:, g % R, :, :], rows(row_no[:, :]), wide(loc[:, g % R, :]), ALU.is_equal)

                LINKS = 4 + 1 if windows else 2 * 4

                def prep(n, s, g):
                    count = [0]

                    def after(ins):
                        count[0] += 1
                        ins.then_inc(s_link, 1)
                        dve.wait_ge(s_link, n * LINKS + count[0])

                    for side in range(2):
                        dve.wait_ge(s_bc[side], 16 * (s + 1))
                    dve.wait_ge(s_B, n + 1)
                    last = dedup(SRC, s, g, after)
                    if windows:
                        in_window(s, g, after)
                        last = v.tensor_scalar(in_winT[:, g % R, :, :], bcast(DST, s, g), base_p[:, ds(s, 1)], None, ALU.is_equal)
                    else:
                        last = dedup(DST, s, g, after)
                    last.then_inc(s_prep, 1)

                def add(n, s, g):
                    dve.wait_ge(s_pre, n + 1)
                    for side in sides:
                        for c in range(G):
                            dve.wait_ge(s_got[side][g % R][c], 16 * (s * (GS // R) + g // R + 1))
                    acc = pre_sum[:, g % 2, :]
                    ins = v.tensor_tensor(acc, ps_pre[g % 2][:, :],
                                          got[SRC][:, g % R, :, :].rearrange("p c f -> p (c f)"), ALU.add)
                    if not windows:
                        ins.then_inc(s_a, 1)
                        dve.wait_ge(s_a, n + 1)
                        ins = v.tensor_tensor(acc, acc, got[DST][:, g % R, :, :].rearrange("p c f -> p (c f)"), ALU.add)
                    ins.then_inc(s_add, 1)

                def flush(s, signal, total, width, ready, need):
                    first = dve.value_load(base_i[0:1, ds(s, 1)], min_val=0, max_val=N - 1)
                    dve.wait_ge(ready, need)
                    v.tensor_tensor(total[:, ds(first, P)], total[:, ds(first, P)], ps_win[0:width, 0:P], ALU.add).then_inc(signal, 1)

                for g in range(R):
                    copy_idx(0, g, sides, s_idx)
                if windows:
                    dve.sem_inc(s_win_free, 1)
                prep(0, 0, 0)
                with dve.Fori(0, NS - 1) as s:
                    for g in range(GS):
                        n = s * GS + g
                        if g + 1 < GS:
                            prep(n + 1, s, g + 1)
                        else:
                            prep(n + 1, s + 1, 0)
                        add(n, s, g)
                        if g + R < GS:
                            copy_idx(s, g + R, sides, s_idx)
                        else:
                            copy_idx(s + 1, g + R - GS, sides, s_idx)
                    if windows:
                        flush(s, s_win_free, hid_win_sum, HW, s_B, R + (s + 1) * GS)
                s = NS - 1
                for g in range(GS):
                    n = s * GS + g
                    if g + 1 < GS:
                        prep(n + 1, s, g + 1)
                    add(n, s, g)
                    if g + R < GS:
                        copy_idx(s, g + R, sides, s_idx)
                if windows:
                    flush(s, s_win_free, hid_win_sum, HW, s_B, R + NG)

                dve.wait_ge(s_parts, 16 * G)
                link(v.tensor_tensor(parts[:, 0, :, :], parts[:, 0, :, :], parts[:, 1, :, :], ALU.add))
                link(v.tensor_tensor(parts[:, 2, :, :], parts[:, 2, :, :], parts[:, 3, :, :], ALU.add))
                v.tensor_tensor(parts[:, 0, :, :], parts[:, 0, :, :], parts[:, 2, :, :], ALU.add).then_inc(s_psum, 1)
                hid_cols = hid_win_sum[:, :].rearrange("f (p j) -> f j p", j=NB)
                with dve.Fori(0, NPAIR) as q:
                    dve.wait_ge(s_n[0], q + 1)
                    v.tensor_tensor(hT[:, :].rearrange("f (j p) -> f j p", j=2),
                                    ps_pre[0][0:HW, 0:2 * P].rearrange("f (j p) -> f j p", j=2),
                                    hid_cols[:, ds(2 * q, 2), :], ALU.add).then_inc(s_n[1], 1)
                    dve.wait_ge(s_n[6], q + 1)
                    v.tensor_tensor(y[:, ds(2 * q, 2), :], xn[:, ds(2 * q, 2), :],
                                    ps_dd[0][1][:, 0:2 * F].rearrange("p (j f) -> p j f", j=2), ALU.add).then_inc(s_n[7], 1)

                def layer_norm(dest, source, turn):
                    def across(small):
                        return small.rearrange("p (j a) -> p j a", a=1).to_broadcast([P, NB, F])
                    link(v.tensor_reduce(out=stat[:, 0, :], in_=source[:, :, :], axis=AX, op=ALU.add))
                    link(v.tensor_scalar(stat[:, 0, :], stat[:, 0, :], 1.0 / F, None, ALU.mult))
                    link(v.tensor_tensor(centred[:, :, :], source[:, :, :], across(stat[:, 0, :]), ALU.subtract))
                    link(v.tensor_tensor(y2[:, :, :], centred[:, :, :], centred[:, :, :], ALU.mult))
                    v.tensor_reduce(out=stat[:, 1, :], in_=y2[:, :, :], axis=AX, op=ALU.add).then_inc(s_sq, 1)
                    dve.wait_ge(s_sqd, turn)
                    link(v.reciprocal(stat[:, 3, :], stat[:, 2, :]))
                    return v.tensor_tensor(dest[:, :, :], centred[:, :, :], across(stat[:, 3, :]), ALU.mult)

                y2 = cat[:, :, 0:F]
                dve.wait_ge(s_n[7], NPAIR)
                layer_norm(x1, y, 1).then_inc(s_x1, 1)

                LINKS1 = 1 if windows else 4

                def prep1(n, s, g):
                    count = [0]

                    def after(ins):
                        count[0] += 1
                        ins.then_inc(s_link1, 1)
                        dve.wait_ge(s_link1, n * LINKS1 + count[0])

                    dve.wait_ge(s_B1, n + 1)
                    if windows:
                        last = in_window(s, g, after)
                    else:
                        dve.wait_ge(s_bc[DST], 16 * (s + 1 + NS))
                        last = dedup(DST, s, g, after)
                    last.then_inc(s_prep1, 1)

                if windows:
                    dve.sem_inc(s_win1_free, 1)
                for g in range(R):
                    copy_idx(0, g, (SRC,), s_idx1)
                prep1(0, 0, 0)
                with dve.Fori(0, NS - 1) as s:
                    for g in range(GS):
                        n = s * GS + g
                        if g + 1 < GS:
                            prep1(n + 1, s, g + 1)
                        else:
                            prep1(n + 1, s + 1, 0)
                        dve.wait_ge(s_B1, R + n + 1)
                        if g + R < GS:
                            copy_idx(s, g + R, (SRC,), s_idx1)
                        else:
                            copy_idx(s + 1, g + R - GS, (SRC,), s_idx1)
                    if windows:
                        flush(s, s_win1_free, nei_win_sum, SW, s_B1, R + (s + 1) * GS)
                s = NS - 1
                for g in range(GS):
                    n = s * GS + g
                    if g + 1 < GS:
                        prep1(n + 1, s, g + 1)
                    dve.wait_ge(s_B1, R + n + 1)
                    if g + R < GS:
                        copy_idx(s, g + R, (SRC,), s_idx1)
                if windows:
                    flush(s, s_win1_free, nei_win_sum, SW, s_B1, R + NG)
                    link(v.memset(parts[:, 0, :, 0:SW], 0.0))
                else:
                    dve.wait_ge(s_parts1, 16 * G)
                    link(v.tensor_tensor(parts[:, 0, :, 0:SW], parts[:, 0, :, 0:SW], parts[:, 1, :, 0:SW], ALU.add))
                    link(v.tensor_tensor(parts[:, 2, :, 0:SW], parts[:, 2, :, 0:SW], parts[:, 3, :, 0:SW], ALU.add))
                    link(v.tensor_tensor(parts[:, 0, :, 0:SW], parts[:, 0, :, 0:SW], parts[:, 2, :, 0:SW], ALU.add))
                v.tensor_copy(cat[:, :, 0:F], x1[:, :, :]).then_inc(s_m[8], 1)
                with dve.Fori(0, NPAIR) as q:
                    dve.wait_ge(s_m[0], q + 1)
                    pair = parts[:, 0, ds(2 * q, 2), 0:SW]
                    v.tensor_tensor(parts[:, 1, ds(2 * q, 2), 0:SW], pair,
                                    ps_pre[0][:, 0:2 * SW].rearrange("p (j f) -> p j f", j=2), ALU.add).then_inc(s_m[1], 1)
                dve.wait_ge(s_m[1], NPAIR)
                link(v.tensor_scalar(stat[:, 0:1, :].rearrange("p a j -> p j a"), parts[:, 1, :, F:SW], 1.0, None, ALU.max))
                link(v.reciprocal(stat[:, 1, :], stat[:, 0, :]))
                v.tensor_tensor(cat[:, :, F:2 * F], parts[:, 1, :, 0:F],
                                stat[:, 1, :].rearrange("p (j a) -> p j a", a=1).to_broadcast([P, NB, F]), ALU.mult).then_inc(s_m[2], 1)
                dve.wait_ge(s_m[6], NPAIR)
                dve.wait_ge(s_m[2], 1)
                link(v.tensor_tensor(y[:, :, :], y[:, :, :], x1[:, :, :], ALU.add))
                layer_norm(y, y, 2).then_inc(s_m[9], 1)

            with dve.If(fast == 1):
                program(True)
            with dve.Else():
                program(False)

        @block.tensor
        def _(pe):
            pe.wait_ge(s_const, 1)
            pe.wait_ge(s_w, 16 * W_DMAS)
            pe.wait_ge(s_x, 32)
            for q in range(NPAIR):
                for j in range(2):
                    last = nc.tensor.transpose(ps_eaT[0:F, j * P:(j + 1) * P], xn[:, 2 * q + j, :], ident[:, :])
                last.then_inc(s_xT, 1)
                pe.wait_ge(s_xTc, q + 1)
                pe.wait_ge(s_rowsc, q + 1)
                for j in range(2):
                    last = nc.tensor.matmul(ps_pre[0][:, j * 4 * HID:(j + 1) * 4 * HID], nT[0:F + 1, j * P:(j + 1) * P],
                                            Wends[:, :], start=True, stop=True)
                last.then_inc(s_rows, 1)
            pe.wait_ge(s_reach, 1)
            nc.tensor.matmul(ps_win[0:1, 0:1], reach[:, 3:4], ones[:, 0:1], start=True, stop=True).then_inc(s_far, 1)
            pe.wait_ge(s_flag, 1)
            fast = pe.value_load(flag[0:1, 0:1], min_val=0, max_val=1)

            def program(windows):
                sides = (SRC,) if windows else (SRC, DST)
                pe.sem_inc(s_B, R)
                pe.sem_inc(s_B1, R)
                pe.sem_inc(s_T, R)

                def ea_T(n, s, g):
                    loads = s * (GS // R) + g // R + 1
                    if isinstance(s, int) and s == NS - 1:
                        loads += g // R + 1
                    pe.wait_ge(s_ea[g % R], 16 * loads)
                    if windows and g == 0:
                        pe.wait_ge(s_win_in, 16 * (s + 1))
                    pe.nop(nofuse=True)
                    nc.tensor.transpose(
                        ps_eaT[0:G * FE, 0:P],
                        ea_in[g % R][:, :, :].rearrange("p c f -> p (c f)"), ident[:, :]).then_inc(s_T, 1)

                def pre(n, s, g):
                    pe.wait_ge(s_Tc, n + 1)
                    if windows:
                        pe.wait_ge(s_prep, n + 1)
                    last = nc.tensor.matmul(ps_pre[g % 2][:, :], eaT[:, g % 2, :],
                                            Cblk[:, :, :].rearrange("k c f -> k (c f)"), start=True, stop=not windows)
                    if windows:
                        for c in range(G):
                            last = nc.tensor.matmul(ps_pre[g % 2][:, c * 2 * HID:(c + 1) * 2 * HID], in_winT[:, g % R, c, :],
                                                    win_rows[:, ds(s % 2, 1), :].rearrange("p a f -> p (a f)"),
                                                    start=False, stop=c == G - 1)
                    last.then_inc(s_pre, 1)

                def use(n, s, g):
                    pe.wait_ge(s_hid, n + 1)
                    pe.wait_ge(s_prep, n + 1)
                    if windows:
                        if g == 0:
                            pe.wait_ge(s_win_free, s + 1)
                        for c in range(G):
                            nc.tensor.matmul(ps_win[0:HW, 0:P], hid[:, g % 2, c, 0:HW], in_win[:, g % R, c, :],
                                             start=g == 0 and c == 0, stop=g == GS - 1 and c == G - 1)
                    for side in sides:
                        for c in range(G):
                            h0 = HW * (1 - side)
                            last = nc.tensor.matmul(ps_dd[side][g % 2][:, c * HW:(c + 1) * HW], same[side][:, g % R, c, :],
                                                    hid[:, g % 2, c, h0:h0 + HW], start=True, stop=True)
                    last.then_inc(s_B, 1)

                ea_T(0, 0, 0)
                pre(0, 0, 0)
                with pe.Fori(0, NS - 2) as s:
                    for g in range(GS):
                        n = s * GS + g
                        s1, g1 = (s, g + 1) if g + 1 < GS else (s + 1, 0)
                        ea_T(n + 1, s1, g1)
                        use(n, s, g)
                        pre(n + 1, s1, g1)
                for s in (NS - 2, NS - 1):
                    for g in range(GS):
                        n = s * GS + g
                        s1, g1 = (s, g + 1) if g + 1 < GS else (s + 1, 0)
                        if n + 1 < NG:
                            ea_T(n + 1, s1, g1)
                        use(n, s, g)
                        if n + 1 < NG:
                            pre(n + 1, s1, g1)

                pe.wait_ge(s_psum, 1)
                for q in range(NPAIR):
                    for j in range(2):
                        last = nc.tensor.transpose(ps_pre[0][0:HW, j * P:(j + 1) * P],
                                                   parts[:, 0, 2 * q + j, :], ident[:, :])
                    last.then_inc(s_n[0], 1)
                    pe.wait_ge(s_n[1], q + 1)
                    nc.tensor.matmul(ps_pre[1][0:HID, 0:2 * P], Wf2b[:, :], hT[:, :], start=True, stop=True).then_inc(s_n[2], 1)
                    pe.wait_ge(s_n[3], q + 1)
                    nc.tensor.matmul(ps_dd[0][0][0:HID, 0:2 * P], Wn1s[:, :], fT[:, :], start=True, stop=True).then_inc(s_n[4], 1)
                    pe.wait_ge(s_n[5], q + 1)
                    for j in range(2):
                        last = nc.tensor.matmul(ps_dd[0][1][:, j * F:(j + 1) * F], uT[:, j * P:(j + 1) * P], Wn2b[:, :],
                                                start=True, stop=True)
                    last.then_inc(s_n[6], 1)
                    pe.wait_ge(s_n[7], q + 1)

                def use1(n, s, g):
                    pe.wait_ge(s_prep1, n + 1)
                    for c in range(G):
                        pe.wait_ge(s_got1[g % R][c], 16 * (s * (GS // R) + g // R + 1))
                    if windows and g == 0:
                        pe.wait_ge(s_win1_free, s + 1)
                    for c in range(G):
                        if windows:
                            last = nc.tensor.matmul(ps_win[0:SW, 0:P], got1[:, g % R, c, :], in_win[:, g % R, c, :],
                                                    start=g == 0 and c == 0, stop=g == GS - 1 and c == G - 1)
                        else:
                            last = nc.tensor.matmul(ps_dd[DST][g % 2][:, c * SW:(c + 1) * SW], same[DST][:, g % R, c, :],
                                                    got1[:, g % R, c, :], start=True, stop=True)
                    last.then_inc(s_B1, 1)

                with pe.Fori(0, NS) as s:
                    for g in range(GS):
                        if not windows:
                            pe.wait_ge(s_sums1, s * GS + g + 1)
                        use1(s * GS + g, s, g)
                pe.wait_ge(s_m[8], 1)
                sum_cols = nei_win_sum[:, :].rearrange("f (p j) -> f j p", j=NB)
                for q in range(NPAIR):
                    for j in range(2):
                        last = nc.tensor.transpose(ps_pre[0][:, j * SW:(j + 1) * SW],
                                                   sum_cols[:, 2 * q + j, :],
                                                   ident[0:SW, 0:SW])
                    last.then_inc(s_m[0], 1)
                    pe.wait_ge(s_m[1], q + 1)
                pe.wait_ge(s_m[2], 1)
                for q in range(NPAIR):
                    for j in range(2):
                        last = nc.tensor.transpose(ps_pre[1][0:2 * F, j * P:(j + 1) * P],
                                                   cat[:, 2 * q + j, :], ident[:, :])
                    last.then_inc(s_m[3], 1)
                    pe.wait_ge(s_m[4], q + 1)
                    for j in range(2):
                        last = nc.tensor.matmul(ps_dd[0][0][:, j * F:(j + 1) * F], nT[:, j * P:(j + 1) * P], Wb[:, :],
                                                start=True, stop=True)
                    last.then_inc(s_m[5], 1)

            with pe.If(fast == 1):
                program(True)
            with pe.Else():
                program(False)


_INS = ['x', 'src', 'dst', 'edge_attr_16', 'L0_gnn_Wf1', 'L0_gnn_bf1', 'L0_gnn_Wf2', 'L0_gnn_bf2', 'L0_gnn_Wn1',
        'L0_gnn_bn1', 'L0_gnn_Wn2', 'L0_gnn_bn2', 'L1_gnn_W', 'L1_gnn_b']
_OUTS = [((N, F), 'float32')]


def kernel(**inputs):
    import numpy as _np
    import concourse.bacc as _bacc
    from concourse import mybir as _mybir
    from concourse.bass_utils import run_bass_kernel_spmd as _run

    nc = _bacc.Bacc("TRN2", target_bir_lowering=False, num_devices=1)
    arrays, args = {}, []
    for name in _INS:
        a = _np.ascontiguousarray(inputs[name])
        arrays[f"in_{name}_dram"] = a
        args.append(nc.dram_tensor(f"in_{name}_dram", a.shape, _mybir.dt.from_np(a.dtype), kind="ExternalInput").ap())
    for i, (shape, dtype) in enumerate(_OUTS):
        dt = _mybir.dt.from_np(_np.dtype(dtype))
        args.append(nc.dram_tensor(f"out_{i}_dram", shape, dt, kind="ExternalOutput").ap())
    build(nc, *args)
    r = _run(nc, [arrays], core_ids=[0])
    got = tuple(r.results[0][f"out_{i}_dram"] for i in range(len(_OUTS)))
    return got[0]
```

```python
import concourse.bass as bass
from concourse import mybir
from contextlib import ExitStack

P = 128
N, F = 3125, 32
E, FE = 103125, 16
HID = 64
NB = 25
NP = NB * P
NPS = NP + P
PAD_NODE = N
TRASH = N + 1
CHUNKS = [(j, min(4, NB - j)) for j in range(0, NB, 4)]
G = 4
GS = 6
CS = G * GS
ES = CS * P
NS = -(-E // ES)
NG = NS * GS
EP = NS * ES
HW = HID + 1
SW = F + 1
R = 3
PARTS = 3
XW = PARTS * F
BY_PE = (3, 5)
HALF = 13
TC = 102
EPS = 1e-5
FULLX = N // NB
ELAST = E - (NS - 1) * ES
FULLE, RESTE = ELAST // CS, ELAST % CS
assert TRASH + P <= NPS and FULLX * NB == N and NS * CS % TC == 0


def build(nc, x, src, dst, ea, Wf1, bf1, Wf2, bf2, Wn1, bn1, Wn2, bn2, W, b, out):
    fp32, i32, u32 = mybir.dt.float32, mybir.dt.int32, mybir.dt.uint32
    u16, bf16 = mybir.dt.uint16, mybir.dt.bfloat16
    ALU, ACT, AX = mybir.AluOpType, mybir.ActivationFunctionType, mybir.AxisListType.X
    ds = bass.ds
    SRC, DST = 0, 1
    ctx = ExitStack()
    with ctx:
        def sb(name, shape, dt=fp32):
            return ctx.enter_context(nc.sbuf_tensor(name, shape, dt))

        def pb(name, shape):
            return ctx.enter_context(nc.psum_tensor(name, shape, fp32))

        def sem(name):
            return ctx.enter_context(nc.semaphore(name))

        ends_list = [nc.dram_tensor(f"ends_list{i}", (EP,), u16).ap() for i in range(2)]
        row_table = [nc.dram_tensor(f"row_table{i}", (NP, 2 * HID), fp32).ap() for i in range(2)]
        x1_table = nc.dram_tensor("x1_table", (NP, F), fp32).ap()
        hid_sum = [nc.dram_tensor(f"hid_sum{i}", (NPS, HW), fp32).ap() for i in range(G)]
        nei_sum = [nc.dram_tensor(f"nei_sum{i}", (NPS, SW), fp32).ap() for i in range(G)]

        xn = sb("xn", [P, NB, F])
        xparts = sb("xparts", [P, NB, XW], bf16)
        node_no = sb("node_no", [P, NB])
        node_i = sb("node_i", [P, NB], i32)
        total = sb("total", [P, NB, SW])
        x1 = sb("x1", [P, NB, F])
        y = sb("y", [P, NB, F])
        centred = sb("centred", [P, NB, F])
        stat = sb("stat", [P, 4, NB])
        shared = sb("shared", [P, max(G * NB * HW, 2 * NP)])
        tables = shared[:, 0:NB * 4 * HID].rearrange("p (j f) -> p j f", j=NB)
        parts = shared[:, 0:G * NB * HW].rearrange("p (t j f) -> p t j f", t=G, j=NB)
        hid_win_sum = sb("hid_win_sum", [HW, NP])
        nei_part_sum = shared[0:XW + 1, 0:NP]
        nei_win_sum = shared[0:SW, NP:2 * NP]
        Wends = sb("Wends", [F + 1, 4 * HID])
        Wsrc = sb("Wsrc", [XW, 2 * HID])
        fold = sb("fold", [XW + 1, SW])
        Cblk = sb("Cblk", [G * FE, G, 2 * HID])
        Wf2b = sb("Wf2b", [HW, HID])
        Wn1s = sb("Wn1s", [HID, HID])
        bn1s = sb("bn1s", [HID, 1])
        Wn2b = sb("Wn2b", [HID + 1, F])
        Wb = sb("Wb", [2 * F + 1, F])
        eps = sb("eps", [P, 1])
        row_i = sb("row_i", [P, P], i32)
        col_i = sb("col_i", [P, 1], i32)
        row_no = sb("row_no", [P, P])
        col_no = sb("col_no", [P, 1])
        trash = sb("trash", [P, 1])
        below = sb("below", [P, P])
        ident = sb("ident", [P, P])
        ones = sb("ones", [P, 1])
        zrow = sb("zrow", [P, (NB + 1) * HW])
        ends = [sb(f"ends{i}", [P, NS, CS], i32) for i in range(2)]
        base_in = sb("base_in", [P, NS], i32)
        base_i = sb("base_i", [P, NS], i32)
        base = sb("base", [P, NS])
        base_p = sb("base_p", [P, NS])
        local = sb("local", [P, NS, CS])
        ends_f = [sb(f"ends_f{i}", [P, NS * CS]) for i in range(2)]
        ends_T = [sb(f"ends_T{i}", [TC, NS * CS // TC, P], u16) for i in range(2)]
        reach = sb("reach", [P, 4])
        flag = sb("flag", [1, 1], i32)
        ends_bc = [sb(f"ends_bc{i}", [P, 2, ES], u16) for i in range(2)]
        ea_in = [sb(f"ea_in{r}", [P, G, FE]) for r in range(R)]
        win_rows = sb("win_rows", [P, 2, 2 * HID])
        get_idx = [[sb(f"get_idx{i}_{r}", [P, G], u32) for r in range(4)] for i in range(2)]
        put_idx = [[sb(f"put_idx{i}_{r}", [P, G], u32) for r in range(GS)] for i in range(2)]
        got = [sb("got_src", [P, 4, G, 2 * HID]), sb("got_dst", [P, R, G, 2 * HID])]
        got1 = sb("nei_rows", [P, 4, G, SW])
        one_of = sb("one_of", [P, NB, G * P], bf16)
        xs = sb("xs", [XW, G * P])
        xg = sb("xg", [P, G, XW + 1], bf16)
        in_win_b = sb("in_win_b", [P, 2, G, P], bf16)
        same = [sb(f"same{i}", [P, R, G, P]) for i in range(2)]
        earlier = sb("earlier", [P, G, P])
        dup = sb("dup", [P, G])
        shift = sb("shift", [P, G])
        loc = sb("loc", [P, R, G])
        in_win = sb("in_win", [P, R, G, P])
        in_winT = sb("in_winT", [P, R, G, P])
        eaT = sb("eaT", [G * FE, 2, P])
        pre_sum = sb("pre_sum", [P, 2, G * 2 * HID])
        hid = sb("hid", [P, 2, G, 2 * HW])
        sums = [sb(f"sums{i}", [P, 2, G, HW]) for i in range(2)]
        spare = [ends_bc[i][:, :, :].rearrange("p a e -> p (a e)").bitcast(fp32) for i in range(2)]

        def two(room, rows, at):
            return room[0:rows, at:at + 8 * P].rearrange("k (a n) -> k a n", a=2)

        nT, uT, fT = two(spare[0], 2 * F + 1, 0), two(spare[0], HID + 1, 8 * P), two(spare[0], HID, 16 * P)
        xT, hT = two(spare[1], F + 1, 0), two(spare[1], HW, 8 * P)
        cat = zrow[:, 0:NB * 2 * F].rearrange("p (j f) -> p j f", j=NB)

        ps_pre = [pb(f"ps_pre{i}", [P, 512]) for i in range(2)]
        ps_dd = [[pb(f"ps_dd{i}_{j}", [P, 512]) for j in range(2)] for i in range(2)]
        ps_eaT = pb("ps_eaT", [P, 512])
        ps_win = pb("ps_win", [P, 512])

        s_w = sem("weights_in")
        s_x = sem("x_in")
        s_ends = sem("ends_in")
        s_iota = sem("iotas_made")
        s_zero = sem("zeros_made")
        s_const = sem("constants_made")
        s_chain = sem("vector_chain")
        s_xT = sem("xT_made")
        s_xTc = sem("xT_copied")
        s_rows = sem("rows_made")
        s_rowsd = sem("rows_copied_by_dve")
        s_rowsa = sem("rows_copied_by_act")
        s_endsf = sem("ends_as_float")
        s_endsT = sem("ends_transposed")
        s_endsTc = sem("ends_T_copied")
        s_list = sem("ends_lists_written")
        s_xp = sem("x_parts_ready")
        s_tab = sem("row_tables_written")
        s_far = sem("reach_counted")
        s_reach = sem("reach_made")
        s_fold = sem("fold_zeroed")
        s_flag = sem("flag_made")
        s_ea = [sem(f"ea_landed{r}") for r in range(R)]
        s_win_in = sem("win_rows_landed")
        s_bc = [sem(f"ends_bc_landed{i}") for i in range(2)]
        s_idx = sem("get_idx_ready")
        s_got = [[[sem(f"got{i}_{r}_{c}") for c in range(G)] for r in range(4)] for i in range(2)]
        s_link = sem("prep_chain")
        s_prep = sem("prep_ready")
        s_T = sem("eaT_made")
        s_Tc = sem("eaT_copied")
        s_pre = sem("pre_made")
        s_a = sem("add_chain")
        s_add = sem("pre_summed")
        s_one = sem("one_hots_made")
        s_xg = sem("features_gathered")
        s_xgc = sem("features_copied")
        s_one1 = sem("l1_one_hots_made")
        s_xg1 = sem("l1_features_gathered")
        s_xg1c = sem("l1_features_copied")
        s_hid = sem("hid_ready")
        s_B = sem("hid_used")
        s_sums = sem("sums_ready")
        s_sums_free = sem("sums_free")
        s_put = [sem(f"hid_scattered{c}") for c in range(G)]
        s_win_free = sem("ps_win_free")
        s_parts = sem("hid_sums_in")
        s_psum = sem("hid_summed")
        s_n = [sem(f"node_step{i}") for i in range(10)]
        s_ln = sem("layer_norm_chain")
        s_sq = sem("sqrt_asked")
        s_sqd = sem("sqrt_done")
        s_x1 = sem("x1_ready")
        s_x1t = sem("x1_table_written")
        s_idx1 = sem("l1_get_idx_ready")
        s_got1 = [[sem(f"l1_got_{r}_{c}") for c in range(G)] for r in range(4)]
        s_link1 = sem("l1_prep_chain")
        s_prep1 = sem("l1_prep_ready")
        s_B1 = sem("l1_rows_used")
        s_sums1 = sem("l1_sums_ready")
        s_sums1_free = sem("l1_sums_free")
        s_put1 = [sem(f"l1_scattered{c}") for c in range(G)]
        s_win1_free = sem("l1_ps_win_free")
        s_parts1 = sem("l1_sums_in")
        s_m = [sem(f"l1_node_step{i}") for i in range(10)]
        s_out = sem("out_written")

        W_DMAS = 4 + 4 + 2 * G + 2 + 1 + 1 + 2 + 2 + 2 * PARTS
        NC = len(CHUNKS)

        def plan(windows):
            mine = [g for g in range(GS) if not (windows and g in BY_PE)]
            return mine, (4 if len(mine) == 4 else 3)

        def bc_rows(side, s):
            return ends_list[side][ds(s * ES, ES)].rearrange("(a n) -> a n", a=1).to_broadcast([P, ES])

        block = ctx.enter_context(nc.Block())

        @block.sync
        def _(sp):
            sp.wait_ge(s_zero, 1)
            sp.dma_start(xn[0:FULLX, :, :], x.rearrange("(p j) f -> p j f", j=NB)).then_inc(s_x, 16)
            cut0 = (NS - 1) * ES
            cut1 = cut0 + FULLE * CS
            for side, e in ((DST, dst), (SRC, src)):
                sp.dma_start(ends[side][:, 0:NS - 1, :], e[0:cut0].rearrange("(s p c) -> p s c", p=P, c=CS)).then_inc(s_ends, 16)
                sp.dma_start(ends[side][0:FULLE, NS - 1, :], e[cut0:cut1].rearrange("(p c) -> p c", c=CS)).then_inc(s_ends, 16)
                sp.dma_start(ends[side][FULLE:FULLE + 1, NS - 1, 0:RESTE], e[cut1:E].rearrange("(p c) -> p c", p=1)).then_inc(s_ends, 16)
            with nc.allow_non_contiguous_dma(reason="one base per supertile"):
                sp.dma_start(base_in[:, 0:NS - 1], dst[0:cut0].rearrange("(s e) -> e s", e=ES)[0:1, :]
                             .to_broadcast([P, NS - 1])).then_inc(s_ends, 16)
                sp.dma_start(base_in[:, NS - 1:NS], dst[cut0:cut0 + 1].rearrange("(a n) -> a n", a=1)
                             .to_broadcast([P, 1])).then_inc(s_ends, 16)
            sp.wait_ge(s_rowsd, NC)
            sp.wait_ge(s_rowsa, NC - 1)
            for side in range(2):
                lo = 2 * HID * (1 - side)
                sp.dma_start(row_table[side].rearrange("(p j) f -> p j f", j=NB),
                             tables[:, :, lo:lo + 2 * HID]).then_inc(s_tab, 16)
            for side in range(2):
                sp.wait_ge(s_endsTc, 2 * (side + 1))
                sp.dma_start(ends_list[side].rearrange("(t r p) -> r t p", r=TC, p=P), ends_T[side][:, :, :]).then_inc(s_list, 16)
            sp.wait_ge(s_list, 32)
            sp.wait_ge(s_flag, 1)
            fast = sp.value_load(flag[0:1, 0:1], min_val=0, max_val=1)

            def program(windows):
                if windows:
                    sp.wait_ge(s_tab, 32)

                def load_ea(n, s, g):
                    sp.wait_ge(s_T, n + 1)
                    cols = slice(g * G, (g + 1) * G)
                    if isinstance(s, int) and s == NS - 1:
                        first, rest = s * ES, min(G, RESTE - g * G)
                        sp.dma_start(ea_in[g % R][0:FULLE, :, :],
                                     ea[first:first + FULLE * CS, :].rearrange("(p c) f -> p c f", c=CS)[:, cols, :]).then_inc(s_ea[g % R], 16)
                        first += FULLE * CS + g * G
                        sp.dma_start(ea_in[g % R][FULLE:FULLE + 1, 0:rest, :],
                                     ea[first:first + rest, :].rearrange("(p c) f -> p c f", p=1)).then_inc(s_ea[g % R], 16)
                    else:
                        sp.dma_start(ea_in[g % R][:, :, :],
                                     ea[ds(s * ES, ES), :].rearrange("(p c) f -> p c f", c=CS)[:, cols, :]).then_inc(s_ea[g % R], 16)

                def load_supertile(s):
                    if windows:
                        first = sp.value_load(base_i[0:1, ds(s, 1)], min_val=0, max_val=NP - P)
                        sp.dma_start(win_rows[:, ds(s % 2, 1), :].rearrange("p a f -> p (a f)"),
                                     row_table[DST][ds(first, P), :]).then_inc(s_win_in, 16)
                    for side in range(2):
                        sp.dma_start(ends_bc[side][:, ds(s % 2, 1), :].rearrange("p a e -> p (a e)"),
                                     bc_rows(side, s)).then_inc(s_bc[side], 16)

                def supertile(s, first=False):
                    for g in range(GS):
                        load_ea(s * GS + g, s, g)
                        if g == R and not (isinstance(s, int) and s == NS - 1):
                            sp.wait_ge(s_pre, s * GS + 1)
                            sp.wait_ge(s_prep, s * GS + 1)
                            load_supertile(s + 1)

                load_supertile(0)
                with sp.Fori(0, NS - 1) as s:
                    supertile(s)
                supertile(NS - 1)
                puts = NG if windows else 2 * NG
                for t in range(G):
                    sp.wait_ge(s_put[t], 16 * (1 + puts))
                    sp.dma_start(parts[:, t, :, :], hid_sum[t][0:NP, :].rearrange("(p j) f -> p j f", j=NB)).then_inc(s_parts, 16)
                sp.wait_ge(s_x1, 1)
                sp.dma_start(x1_table.rearrange("(p j) f -> p j f", j=NB), x1[:, :, :]).then_inc(s_x1t, 16)
                again = SRC if windows else DST
                sp.wait_ge(s_n[7], NC)
                if windows:
                    sp.wait_ge(s_one, len(BY_PE) * NS * NB)
                sp.dma_start(ends_bc[again][:, 0, :], bc_rows(again, 0)).then_inc(s_bc[again], 16)
                with sp.Fori(1, NS) as s:
                    sp.wait_ge(s_prep1, (s - 1) * GS + 2)
                    if windows:
                        sp.wait_ge(s_one1, (s - 1) * len(BY_PE) * NB + 1)
                    sp.dma_start(ends_bc[again][:, ds(s % 2, 1), :].rearrange("p a e -> p (a e)"), bc_rows(again, s)).then_inc(s_bc[again], 16)
                if not windows:
                    for t in range(G):
                        sp.wait_ge(s_put1[t], 16 * (1 + NG))
                        sp.dma_start(parts[:, t, :, 0:SW], nei_sum[t][0:NP, :].rearrange("(p j) f -> p j f", j=NB)).then_inc(s_parts1, 16)
                sp.wait_ge(s_x1t, 16)
                sp.wait_ge(s_m[9], 1)
                sp.dma_start(out.rearrange("(p j) f -> p j f", j=NB), y[0:FULLX, :, :]).then_inc(s_out, 16)
                sp.wait_ge(s_out, 16)

            with sp.If(fast == 1):
                program(True)
            with sp.Else():
                program(False)

        @block.gpsimd
        def _(pool):
            nc.gpsimd.iota(row_i[:, :], pattern=[[1, P]], base=0, channel_multiplier=0).then_inc(s_iota, 1)
            nc.gpsimd.iota(col_i[:, :], pattern=[[0, 1]], base=0, channel_multiplier=1).then_inc(s_iota, 1)
            nc.gpsimd.iota(node_i[:, :], pattern=[[1, NB]], base=0, channel_multiplier=NB).then_inc(s_iota, 1)
            pool.wait_ge(s_zero, 1)
            for t in range(G):
                pool.dma_start(hid_sum[t].rearrange("(p j) f -> p (j f)", p=P), zrow[:, 0:NPS // P * HW]).then_inc(s_put[t], 16)
            pool.wait_ge(s_tab, 32)
            for t in range(G):
                pool.wait_ge(s_put[t], 16)
            pool.wait_ge(s_flag, 1)
            fast = pool.value_load(flag[0:1, 0:1], min_val=0, max_val=1)

            def program(windows):
                sides = (SRC,) if windows else (SRC, DST)
                if not windows:
                    for t in range(G):
                        pool.dma_start(nei_sum[t].rearrange("(p j) f -> p (j f)", p=P), zrow[:, 0:NPS // P * SW]).then_inc(s_put1[t], 16)
                    for t in range(G):
                        pool.wait_ge(s_put1[t], 16)

                mine, depth = plan(windows)
                k_mine = len(mine)

                def gather(m, o):
                    pool.wait_ge(s_idx, m + 1)
                    pool.nop(nofuse=True)
                    for side in sides:
                        for c in range(G):
                            pool.indirect_dma_start(
                                out=got[side][:, o % depth, c, :], out_offset=None, in_=row_table[side],
                                in_offset=bass.IndirectOffsetOnAxis(ap=get_idx[side][o % depth][:, c:c + 1], axis=0))\
                                .then_inc(s_got[side][o % depth][c], 16)

                def scatter(n, g):
                    pool.wait_ge(s_sums, n + 1)
                    pool.wait_ge(s_prep, n + 1)
                    for c in range(G):
                        pool.wait_ge(s_put[c], 16 * (len(sides) * n + 1))
                    pool.nop(nofuse=True).then_inc(s_sums_free, 1)
                    for j, side in enumerate(sides):
                        for c in range(G):
                            if j:
                                pool.wait_ge(s_put[c], 16 * (len(sides) * n + 2))
                                pool.nop(nofuse=True)
                            pool.indirect_dma_start(
                                out=hid_sum[c], in_=sums[side][:, g % 2, c, :], in_offset=None,
                                out_offset=bass.IndirectOffsetOnAxis(ap=put_idx[side][g][:, c:c + 1], axis=0),
                                compute_op=ALU.add).then_inc(s_put[c], 16)

                pool.sem_inc(s_sums_free, 1)
                gather(0, 0)
                gather(1, 1)

                def step(s, g, gather, scatter):
                    if g in mine:
                        o = mine.index(g)
                        if not (isinstance(s, int) and o + 2 >= k_mine):
                            gather(s * k_mine + o + 2, (o + 2) % k_mine)
                    if scatter:
                        scatter(s * GS + g, g)

                with pool.Fori(0, NS - 1) as s:
                    for g in range(GS):
                        step(s, g, gather, scatter)
                for g in range(GS):
                    step(NS - 1, g, gather, scatter)

                pool.wait_ge(s_x1t, 16)
                if not windows:
                    pool.sem_inc(s_sums1_free, 1)

                def gather1(m, o):
                    pool.wait_ge(s_idx1, m + 1)
                    pool.nop(nofuse=True)
                    for c in range(G):
                        pool.indirect_dma_start(
                            out=got1[:, o % depth, c, 0:F], out_offset=None, in_=x1_table,
                            in_offset=bass.IndirectOffsetOnAxis(ap=get_idx[SRC][o % depth][:, c:c + 1], axis=0))\
                            .then_inc(s_got1[o % depth][c], 16)

                def scatter1(n, g):
                    pool.wait_ge(s_sums1, n + 1 + 2)
                    pool.wait_ge(s_prep1, n + 1)
                    for c in range(G):
                        pool.wait_ge(s_put1[c], 16 * (n + 1))
                    pool.nop(nofuse=True).then_inc(s_sums1_free, 1)
                    for c in range(G):
                        pool.indirect_dma_start(
                            out=nei_sum[c], in_=sums[DST][:, g % 2, c, 0:SW], in_offset=None,
                            out_offset=bass.IndirectOffsetOnAxis(ap=put_idx[DST][g][:, c:c + 1], axis=0),
                            compute_op=ALU.add).then_inc(s_put1[c], 16)

                gather1(0, 0)
                gather1(1, 1)
                with pool.Fori(0, NS - 1) as s:
                    for g in range(GS):
                        step(s, g, gather1, None if windows else scatter1)
                for g in range(GS):
                    step(NS - 1, g, gather1, None if windows else scatter1)

            with pool.If(fast == 1):
                program(True)
            with pool.Else():
                program(False)

        @block.scalar
        def _(act):
            act.wait_ge(s_zero, 1)
            for k in range(4):
                r = F * (k in (1, 2))
                act.dma_start(Wends[0:F, k * HID:(k + 1) * HID], Wf1[r:r + F, :]).then_inc(s_w, 16)
            for k in range(2):
                act.dma_start(Wends[F:F + 1, k * HID:(k + 1) * HID], bf1.rearrange("(a n) -> a n", a=1)).then_inc(s_w, 16)
                act.dma_start(Wends[F:F + 1, (2 + k) * HID:(3 + k) * HID], zrow[0:1, 0:HID]).then_inc(s_w, 16)
            for t in range(PARTS):
                for k in range(2):
                    act.dma_start(Wsrc[t * F:(t + 1) * F, k * HID:(k + 1) * HID], Wf1[F * (1 - k):F * (2 - k), :]).then_inc(s_w, 16)
            for c in range(G):
                for k in range(2):
                    act.dma_start(Cblk[c * FE:(c + 1) * FE, c, k * HID:(k + 1) * HID], Wf1[2 * F:2 * F + FE, :]).then_inc(s_w, 16)
            act.dma_start(Wf2b[0:HID, :], Wf2).then_inc(s_w, 16)
            act.dma_start(Wf2b[HID:HW, :], bf2.rearrange("(a n) -> a n", a=1)).then_inc(s_w, 16)
            act.dma_start(Wn1s[:, :], Wn1).then_inc(s_w, 16)
            act.dma_start(bn1s[:, :], bn1.rearrange("(n a) -> n a", a=1)).then_inc(s_w, 16)
            act.dma_start(Wn2b[0:HID, :], Wn2).then_inc(s_w, 16)
            act.dma_start(Wn2b[HID:HID + 1, :], bn2.rearrange("(a n) -> a n", a=1)).then_inc(s_w, 16)
            act.dma_start(Wb[0:2 * F, :], W).then_inc(s_w, 16)
            act.dma_start(Wb[2 * F:2 * F + 1, :], b.rearrange("(a n) -> a n", a=1)).then_inc(s_w, 16)
            def copy_xT(q):
                act.wait_ge(s_xT, q + 1)
                w = CHUNKS[q][1] * P
                nc.scalar.activation(xT[0:F, q % 2, 0:w], (ps_eaT, ps_win)[q % 2][0:F, 0:w], ACT.Copy).then_inc(s_xTc, 1)

            copy_xT(0)
            for q, (j0, nj) in enumerate(CHUNKS):
                if q + 1 < NC:
                    copy_xT(q + 1)
                if nj > 2:
                    act.wait_ge(s_rows, q + 1)
                    nc.scalar.activation(tables[:, j0 + 2:j0 + nj, :],
                                         (ps_pre[1], ps_dd[SRC][1])[q % 2][:, 0:(nj - 2) * 4 * HID]
                                         .rearrange("p (j f) -> p j f", f=4 * HID), ACT.Copy).then_inc(s_rowsa, 1)
            for side in range(2):
                for h in range(2):
                    act.wait_ge(s_endsT, 2 * side + h + 1)
                    nc.scalar.activation(ends_T[side][:, 4 * h:4 * h + 4, :],
                                         (ps_pre[0], ps_pre[1])[h][0:TC, :].rearrange("r (t p) -> r t p", t=4), ACT.Copy).then_inc(s_endsTc, 1)
            act.wait_ge(s_flag, 1)
            fast = act.value_load(flag[0:1, 0:1], min_val=0, max_val=1)

            def program(windows):
                sides = (SRC,) if windows else (SRC, DST)

                def copy_eaT(n, g):
                    act.wait_ge(s_T, R + n + 1)
                    nc.scalar.activation(eaT[:, g % 2, :], ps_eaT[0:G * FE, 0:P], ACT.Copy).then_inc(s_Tc, 1)

                mine, depth = plan(windows)
                k_mine = len(mine)

                def relu(n, s, g):
                    if g in mine:
                        act.wait_ge(s_add, s * k_mine + mine.index(g) + 1)
                        before = pre_sum[:, g % 2, :]
                    else:
                        act.wait_ge(s_pre, n + 1)
                        before = ps_pre[g % 2][:, :]
                    nc.scalar.activation(
                        hid[:, g % 2, :, :].rearrange("p c (k f) -> p c k f", k=2)[:, :, :, 0:HID],
                        before.rearrange("p (c k f) -> p c k f", c=G, k=2), ACT.Relu).then_inc(s_hid, 1)

                def copy_xs(s, g):
                    act.wait_ge(s_xg, s * len(BY_PE) + BY_PE.index(g) + 1 + 1)
                    nc.scalar.activation(xs[:, :], ps_dd[DST][0][0:XW, :], ACT.Copy).then_inc(s_xgc, 1)

                def copy_sums(n, g):
                    act.wait_ge(s_B, R + n + 1)
                    act.wait_ge(s_sums_free, n + 1)
                    for side in sides:
                        last = nc.scalar.activation(
                            sums[side][:, g % 2, :, :],
                            ps_dd[side][g % 2][:, 0:G * HW].rearrange("p (c f) -> p c f", c=G), ACT.Copy)
                    last.then_inc(s_sums, 1)

                copy_eaT(0, 0)
                copy_eaT(1, 1)

                def step(s, g):
                    n = s * GS + g
                    if g + 1 < GS and g + 1 not in mine:
                        copy_xs(s, g + 1)
                    relu(n, s, g)
                    if not (isinstance(s, int) and g + 2 >= GS):
                        copy_eaT(n + 2, (g + 2) % GS)
                    copy_sums(n, g)

                with act.Fori(0, NS - 1) as s:
                    for g in range(GS):
                        step(s, g)
                for g in range(GS):
                    step(NS - 1, g)
                for t in range(NC + 2):
                    if 1 <= t <= NC:
                        q = t - 1
                        w = CHUNKS[q][1] * P
                        act.wait_ge(s_n[2], q + 1)
                        nc.scalar.activation(fT[:, q % 2, 0:w], ps_dd[0][q % 2][0:HID, 0:w], ACT.Copy).then_inc(s_n[3], 1)
                    if 2 <= t:
                        q = t - 2
                        w = CHUNKS[q][1] * P
                        act.wait_ge(s_n[4], q + 1)
                        nc.scalar.activation(uT[0:HID, q % 2, 0:w], ps_dd[1][q % 2][0:HID, 0:w], ACT.Relu, bias=bn1s[:, 0:1]).then_inc(s_n[5], 1)
                act.wait_ge(s_sq, 1)
                nc.scalar.activation(stat[:, 2, :], stat[:, 1, :], ACT.Sqrt, bias=eps[:, 0:1], scale=1.0 / F).then_inc(s_sqd, 1)
                if not windows:
                    act.sem_inc(s_sums1, 2)

                    def copy_sums1(n, g):
                        act.wait_ge(s_B1, R + n + 1)
                        act.wait_ge(s_sums1_free, n + 1)
                        nc.scalar.activation(
                            sums[DST][:, g % 2, :, 0:SW],
                            ps_dd[DST][g % 2][:, 0:G * SW].rearrange("p (c f) -> p c f", c=G), ACT.Copy).then_inc(s_sums1, 1)
                    with act.Fori(0, NS) as s:
                        for g in range(GS):
                            copy_sums1(s * GS + g, g)
                if windows:
                    def copy_xg(s, g):
                        act.wait_ge(s_xg1, s * len(BY_PE) + BY_PE.index(g) + 1 + 1)
                        if g == BY_PE[0]:
                            act.wait_ge(s_B1, R + s * GS + 1)
                        else:
                            act.wait_ge(s_B1, R + s * GS + BY_PE[0] + 1)
                        nc.scalar.activation(xg[:, :, 0:XW], ps_dd[DST][BY_PE.index(g)][:, 0:G * XW].rearrange("p (c f) -> p c f", c=G),
                                             ACT.Copy).then_inc(s_xg1c, 1)

                    with act.Fori(0, NS) as s:
                        for g in BY_PE:
                            copy_xg(s, g)
                for q, (j0, nj) in enumerate(CHUNKS):
                    act.wait_ge(s_m[3], q + 1)
                    nc.scalar.activation(nT[0:2 * F, q % 2, 0:nj * P], ps_pre[q % 2][0:2 * F, 0:nj * P], ACT.Copy).then_inc(s_m[4], 1)
                act.wait_ge(s_sq, 2)
                nc.scalar.activation(stat[:, 2, :], stat[:, 1, :], ACT.Sqrt, bias=eps[:, 0:1], scale=1.0 / F).then_inc(s_sqd, 1)

            with act.If(fast == 1):
                program(True)
            with act.Else():
                program(False)

        @block.vector
        def _(dve):
            chain = [0]

            def link(ins):
                chain[0] += 1
                ins.then_inc(s_chain, 1)
                dve.wait_ge(s_chain, chain[0])

            v = nc.vector
            v.memset(ends[DST][:, NS - 1, :], PAD_NODE)
            v.memset(ends[SRC][:, NS - 1, :], PAD_NODE)
            v.memset(xn[96:P, :, :], 0.0)
            v.memset(Cblk[:, :, :], 0.0)
            v.memset(zrow[:, :], 0.0).then_inc(s_zero, 1)
            v.memset(xT[F:F + 1, :, :], 1.0)
            v.memset(ones[:, :], 1.0)
            v.memset(eps[:, :], EPS)
            v.memset(xg[:, :, XW:XW + 1], 1.0)
            v.memset(got1[:, :, :, F:SW], 1.0)
            for k in range(2):
                v.memset(hid[:, :, :, k * HW + HID:(k + 1) * HW], 1.0)
            dve.wait_ge(s_iota, 3)
            v.tensor_copy(row_no[:, :], row_i[:, :])
            v.tensor_copy(node_no[:, :], node_i[:, :])
            link(v.tensor_copy(col_no[:, :], col_i[:, :]))
            v.tensor_scalar(trash[:, :], col_no[:, :], float(TRASH), None, ALU.add)
            v.tensor_scalar(below[:, :], row_no[:, :], col_no[:, 0:1], None, ALU.is_lt)
            v.tensor_scalar(ident[:, :], row_no[:, :], col_no[:, 0:1], None, ALU.is_equal).then_inc(s_const, 1)
            for q, (j0, nj) in enumerate(CHUNKS):
                dve.wait_ge(s_rows, q + 1)
                w = min(nj, 2)
                v.tensor_copy(tables[:, j0:j0 + w, :], (ps_pre[0], ps_dd[SRC][0])[q % 2][:, 0:w * 4 * HID]
                              .rearrange("p (j f) -> p j f", f=4 * HID)).then_inc(s_rowsd, 1)
            dve.wait_ge(s_ends, 16 * 8)
            for side in range(2):
                v.tensor_copy(ends_f[side][:, :], ends[side][:, :, :].rearrange("p s c -> p (s c)")).then_inc(s_endsf, 1)
            v.memset(hid_win_sum[:, :], 0.0)
            link(v.tensor_scalar(base[:, :], base_in[:, :], float(NP - P), None, ALU.min))
            v.tensor_copy(base_i[:, :], base[:, :])
            v.tensor_scalar(base_p[:, :], base[:, :], col_no[:, 0:1], None, ALU.add)
            link(v.tensor_tensor(local[:, :, :], ends[DST][:, :, :],
                                 base[:, :].rearrange("p (s a) -> p s a", a=1).to_broadcast([P, NS, CS]), ALU.subtract))
            flat = local[:, :, :].rearrange("p s c -> p (s c)")
            v.tensor_reduce(out=reach[:, 0:1], in_=flat, axis=AX, op=ALU.max)
            link(v.tensor_reduce(out=reach[:, 1:2], in_=flat, axis=AX, op=ALU.min))
            v.tensor_scalar(reach[:, 2:3], reach[:, 0:1], P - 0.5, None, ALU.is_gt)
            link(v.tensor_scalar(reach[:, 1:2], reach[:, 1:2], -0.5, None, ALU.is_lt))
            v.tensor_tensor(reach[:, 3:4], reach[:, 1:2], reach[:, 2:3], ALU.add).then_inc(s_reach, 1)
            dve.wait_ge(s_far, 1)
            v.tensor_scalar(flag[:, :], ps_win[0:1, 0:1], 0.5, None, ALU.is_lt).then_inc(s_flag, 1)
            def split(source):
                link(v.tensor_copy(xparts[:, :, 0:F], source[:, :, :]))
                link(v.tensor_tensor(centred[:, :, :], source[:, :, :], xparts[:, :, 0:F], ALU.subtract))
                link(v.tensor_copy(xparts[:, :, F:2 * F], centred[:, :, :]))
                link(v.tensor_tensor(centred[:, :, :], centred[:, :, :], xparts[:, :, F:2 * F], ALU.subtract))
                return v.tensor_copy(xparts[:, :, 2 * F:3 * F], centred[:, :, :])

            split(xn).then_inc(s_xp, 1)
            v.memset(fold[:, :], 0.0).then_inc(s_fold, 1)
            dve.wait_ge(s_fold, 1)
            for t in range(PARTS):
                v.tensor_copy(fold[t * F:(t + 1) * F, 0:F], ident[t * F:(t + 1) * F, t * F:(t + 1) * F])
            v.memset(fold[XW:XW + 1, F:SW], 1.0)
            dve.wait_ge(s_flag, 1)
            fast = dve.value_load(flag[0:1, 0:1], min_val=0, max_val=1)

            before = chain[0]

            def program(windows):
                chain[0] = before
                sides = (SRC,) if windows else (SRC, DST)

                mine, depth = plan(windows)
                k_mine = len(mine)

                def copy_idx(s, o, which, signal):
                    for side in which:
                        last = v.tensor_copy(get_idx[side][o % depth][:, :], col(side, s, mine[o]))
                    last.then_inc(signal, 1)

                def col(side, s, g):
                    return ends[side][:, ds(s, 1), g * G:(g + 1) * G].rearrange("p a c -> p (a c)")

                def bcast(side, s, g):
                    return ends_bc[side][:, ds(s % 2, 1), g * G * P:(g + 1) * G * P].rearrange("p a (c q) -> p (a c) q", q=P)

                def wide(small):
                    return small.rearrange("p (c a) -> p c a", a=1).to_broadcast([P, G, P])

                def rows(small):
                    return small.rearrange("p (a q) -> p a q", a=1).to_broadcast([P, G, P])

                def dedup(side, s, g, after):
                    after(v.tensor_tensor(same[side][:, g % R, :, :], bcast(side, s, g), wide(col(side, s, g)), ALU.is_equal))
                    after(v.tensor_tensor(earlier[:, :, :], same[side][:, g % R, :, :], rows(below[:, :]), ALU.mult))
                    v.tensor_scalar(shift[:, :], col(side, s, g), -1.0, trash[:, 0:1], ALU.mult, ALU.add)
                    after(v.tensor_reduce(out=dup[:, :], in_=earlier[:, :, :], axis=AX, op=ALU.max))
                    after(v.tensor_tensor(shift[:, :], shift[:, :], dup[:, :], ALU.mult))
                    return v.tensor_tensor(put_idx[side][g][:, :], shift[:, :], col(side, s, g), ALU.add)

                def in_window(s, g, after, to):
                    after(v.tensor_scalar(loc[:, g % R, :], col(DST, s, g), base[:, ds(s, 1)], None, ALU.subtract))
                    return v.tensor_tensor(to, rows(row_no[:, :]), wide(loc[:, g % R, :]), ALU.is_equal)

                LINKS = 4 + 1 if windows else 2 * 4

                def prep(n, s, g):
                    count = [0]

                    def after(ins):
                        count[0] += 1
                        ins.then_inc(s_link, 1)
                        dve.wait_ge(s_link, n * LINKS + count[0])

                    for side in range(2):
                        dve.wait_ge(s_bc[side], 16 * (s + 1))
                    dve.wait_ge(s_B, n + 1)
                    last = dedup(SRC, s, g, after)
                    if windows:
                        in_window(s, g, after, in_win[:, g % R, :, :])
                        last = v.tensor_scalar(in_winT[:, g % R, :, :], bcast(DST, s, g), base_p[:, ds(s, 1)], None, ALU.is_equal)
                    else:
                        last = dedup(DST, s, g, after)
                    last.then_inc(s_prep, 1)

                def add(n, s, g):
                    o = mine.index(g)
                    dve.wait_ge(s_pre, n + 1)
                    for side in sides:
                        for c in range(G):
                            dve.wait_ge(s_got[side][o % depth][c], 16 * (s * (k_mine // depth) + o // depth + 1))
                    acc = pre_sum[:, g % 2, :]
                    ins = v.tensor_tensor(acc, ps_pre[g % 2][:, :],
                                          got[SRC][:, o % depth, :, :].rearrange("p c f -> p (c f)"), ALU.add)
                    if not windows:
                        ins.then_inc(s_a, 1)
                        dve.wait_ge(s_a, n + 1)
                        ins = v.tensor_tensor(acc, acc, got[DST][:, o % depth, :, :].rearrange("p c f -> p (c f)"), ALU.add)
                    ins.then_inc(s_add, 1)

                def flush(s, signal, sums_of, ready, need):
                    first = dve.value_load(base_i[0:1, ds(s, 1)], min_val=0, max_val=NP - P)
                    dve.wait_ge(ready, need)
                    for whole, bank, width in sums_of:
                        last = v.tensor_tensor(whole[0:width, ds(first, P)], whole[0:width, ds(first, P)], bank[0:width, 0:P], ALU.add)
                    last.then_inc(signal, 1)

                def one_hots(s, g, half, used, made):
                    turn = s * len(BY_PE) + BY_PE.index(g)
                    if half == 0:
                        dve.wait_ge(used, turn + 1)
                    for j in range(half * HALF, NB if half else HALF):
                        v.tensor_scalar(one_of[:, j, :],
                                        ends_bc[SRC][:, ds(s % 2, 1), g * G * P:(g + 1) * G * P].rearrange("p a e -> p (a e)"),
                                        node_no[:, j:j + 1], None, ALU.is_equal).then_inc(made, 1)

                def ahead(s, g, used, made):
                    if windows:
                        for half in range(2):
                            if g + 3 - half in BY_PE:
                                one_hots(s, g + 3 - half, half, used, made)

                def next_idx(s, g, which, signal):
                    o = mine.index(g) + depth
                    if o < k_mine:
                        copy_idx(s, o, which, signal)
                    elif not (isinstance(s, int) and s == NS - 1):
                        copy_idx(s + 1, o - k_mine, which, signal)

                for o in range(depth):
                    copy_idx(0, o, sides, s_idx)
                if windows:
                    dve.sem_inc(s_win_free, 1)
                prep(0, 0, 0)

                def step(s, g):
                    n = s * GS + g
                    if g + 1 < GS:
                        prep(n + 1, s, g + 1)
                    elif not (isinstance(s, int) and s == NS - 1):
                        prep(n + 1, s + 1, 0)
                    if g in mine:
                        add(n, s, g)
                        next_idx(s, g, sides, s_idx)
                    ahead(s, g, s_xg, s_one)

                with dve.Fori(0, NS - 1) as s:
                    for g in range(GS):
                        step(s, g)
                    if windows:
                        flush(s, s_win_free, [(hid_win_sum, ps_win, HW)], s_B, R + (s + 1) * GS)
                for g in range(GS):
                    step(NS - 1, g)
                if windows:
                    flush(NS - 1, s_win_free, [(hid_win_sum, ps_win, HW)], s_B, R + NG)

                v.memset(uT[HID:HID + 1, :, :], 1.0)
                dve.wait_ge(s_parts, 16 * G)
                link(v.tensor_tensor(parts[:, 0, :, :], parts[:, 0, :, :], parts[:, 1, :, :], ALU.add))
                link(v.tensor_tensor(parts[:, 2, :, :], parts[:, 2, :, :], parts[:, 3, :, :], ALU.add))
                v.tensor_tensor(parts[:, 0, :, :], parts[:, 0, :, :], parts[:, 2, :, :], ALU.add).then_inc(s_psum, 1)
                hid_cols = hid_win_sum[:, :].rearrange("f (p j) -> f j p", j=NB)
                for t in range(NC + 3):
                    if t < NC:
                        j0, nj = CHUNKS[t]
                        dve.wait_ge(s_n[0], t + 1)
                        v.tensor_tensor(hT[:, t % 2, 0:nj * P].rearrange("f (j p) -> f j p", j=nj),
                                        ps_pre[t % 2][0:HW, 0:nj * P].rearrange("f (j p) -> f j p", j=nj),
                                        hid_cols[:, j0:j0 + nj, :], ALU.add).then_inc(s_n[1], 1)
                    if t >= 3:
                        j0, nj = CHUNKS[t - 3]
                        dve.wait_ge(s_n[6], t - 2)
                        v.tensor_tensor(y[:, j0:j0 + nj, :], xn[:, j0:j0 + nj, :],
                                        (ps_eaT, ps_win)[(t - 3) % 2][:, 0:nj * F].rearrange("p (j f) -> p j f", j=nj),
                                        ALU.add).then_inc(s_n[7], 1)

                def layer_norm(dest, source, turn):
                    def across(small):
                        return small.rearrange("p (j a) -> p j a", a=1).to_broadcast([P, NB, F])
                    link(v.tensor_reduce(out=stat[:, 0, :], in_=source[:, :, :], axis=AX, op=ALU.add))
                    link(v.tensor_scalar(stat[:, 0, :], stat[:, 0, :], 1.0 / F, None, ALU.mult))
                    link(v.tensor_tensor(centred[:, :, :], source[:, :, :], across(stat[:, 0, :]), ALU.subtract))
                    link(v.tensor_tensor(y2[:, :, :], centred[:, :, :], centred[:, :, :], ALU.mult))
                    v.tensor_reduce(out=stat[:, 1, :], in_=y2[:, :, :], axis=AX, op=ALU.add).then_inc(s_sq, 1)
                    dve.wait_ge(s_sqd, turn)
                    link(v.reciprocal(stat[:, 3, :], stat[:, 2, :]))
                    return v.tensor_tensor(dest[:, :, :], centred[:, :, :], across(stat[:, 3, :]), ALU.mult)

                y2 = cat[:, :, 0:F]
                dve.wait_ge(s_n[7], NC)
                layer_norm(x1, y, 1).then_inc(s_x1, 1)
                if windows:
                    dve.wait_ge(s_x1, 1)
                    split(x1).then_inc(s_xp, 1)
                    v.memset(shared[0:XW + 1, 0:2 * NP], 0.0)

                LINKS1 = 1 if windows else 4

                def prep1(n, s, g):
                    count = [0]

                    def after(ins):
                        count[0] += 1
                        ins.then_inc(s_link1, 1)
                        dve.wait_ge(s_link1, n * LINKS1 + count[0])

                    dve.wait_ge(s_B1, n + 1)
                    if windows:
                        last = in_window(s, g, after, in_win[:, g % R, :, :] if g in mine else in_win_b[:, BY_PE.index(g), :, :])
                    else:
                        dve.wait_ge(s_bc[DST], 16 * (s + 1 + NS))
                        last = dedup(DST, s, g, after)
                    last.then_inc(s_prep1, 1)

                if windows:
                    dve.sem_inc(s_win1_free, 1)
                for o in range(depth):
                    copy_idx(0, o, (SRC,), s_idx1)
                prep1(0, 0, 0)

                def step1(s, g):
                    n = s * GS + g
                    if g + 1 < GS:
                        prep1(n + 1, s, g + 1)
                    elif not (isinstance(s, int) and s == NS - 1):
                        prep1(n + 1, s + 1, 0)
                    if windows and g == 0:
                        dve.wait_ge(s_bc[SRC], 16 * (s + 1 + NS))
                    ahead(s, g, s_xg1, s_one1)
                    if g in mine:
                        dve.wait_ge(s_B1, R + n + 1)
                        next_idx(s, g, (SRC,), s_idx1)

                win1_sums = [(nei_win_sum, ps_win, SW), (nei_part_sum, ps_dd[SRC][1], XW + 1)]
                with dve.Fori(0, NS - 1) as s:
                    for g in range(GS):
                        step1(s, g)
                    if windows:
                        flush(s, s_win1_free, win1_sums, s_B1, R + (s + 1) * GS)
                for g in range(GS):
                    step1(NS - 1, g)
                if windows:
                    flush(NS - 1, s_win1_free, win1_sums, s_B1, R + NG)
                    for h, (j0, nj) in enumerate(((0, 15), (15, 10))):
                        dve.wait_ge(s_m[0], h + 1)
                        v.tensor_copy(total[:, j0:j0 + nj, :],
                                      ps_pre[h][:, 0:nj * SW].rearrange("p (j f) -> p j f", j=nj)).then_inc(s_m[1], 1)
                else:
                    dve.wait_ge(s_parts1, 16 * G)
                    link(v.tensor_tensor(parts[:, 0, :, 0:SW], parts[:, 0, :, 0:SW], parts[:, 1, :, 0:SW], ALU.add))
                    link(v.tensor_tensor(parts[:, 2, :, 0:SW], parts[:, 2, :, 0:SW], parts[:, 3, :, 0:SW], ALU.add))
                    v.tensor_tensor(total[:, :, :], parts[:, 0, :, 0:SW], parts[:, 2, :, 0:SW], ALU.add).then_inc(s_m[1], 2)
                v.memset(nT[2 * F:2 * F + 1, :, :], 1.0)
                dve.wait_ge(s_m[1], 2)
                v.tensor_copy(cat[:, :, 0:F], x1[:, :, :])
                link(v.tensor_scalar(stat[:, 0:1, :].rearrange("p a j -> p j a"), total[:, :, F:SW], 1.0, None, ALU.max))
                link(v.reciprocal(stat[:, 1, :], stat[:, 0, :]))
                v.tensor_tensor(cat[:, :, F:2 * F], total[:, :, 0:F],
                                stat[:, 1, :].rearrange("p (j a) -> p j a", a=1).to_broadcast([P, NB, F]), ALU.mult).then_inc(s_m[2], 1)
                for h, (j0, nj) in enumerate(((0, 16), (16, 9))):
                    dve.wait_ge(s_m[5], h + 1)
                    ins = v.scalar_tensor_tensor(y[:, j0:j0 + nj, :], ps_dd[1][h][:, 0:nj * F].rearrange("p (j f) -> p j f", j=nj),
                                                 0.0, x1[:, j0:j0 + nj, :], ALU.max, ALU.add)
                link(ins)
                layer_norm(y, y, 2).then_inc(s_m[9], 1)

            with dve.If(fast == 1):
                program(True)
            with dve.Else():
                program(False)

        @block.tensor
        def _(pe):
            pe.wait_ge(s_const, 1)
            pe.wait_ge(s_w, 16 * W_DMAS)
            pe.wait_ge(s_x, 16)
            def x_T(q):
                j0, nj = CHUNKS[q]
                for j in range(nj):
                    last = nc.tensor.transpose((ps_eaT, ps_win)[q % 2][0:F, j * P:(j + 1) * P], xn[:, j0 + j, :], ident[:, :])
                last.then_inc(s_xT, 1)

            x_T(0)
            for q, (j0, nj) in enumerate(CHUNKS):
                if q + 1 < NC:
                    x_T(q + 1)
                pe.wait_ge(s_xTc, q + 1)
                if q >= 2:
                    pe.wait_ge(s_rowsd, q - 1)
                    pe.wait_ge(s_rowsa, q - 1)
                for j in range(nj):
                    bank = ((ps_pre, ps_dd[SRC])[q % 2])[j // 2]
                    last = nc.tensor.matmul(bank[:, j % 2 * 4 * HID:(j % 2 + 1) * 4 * HID],
                                            xT[:, q % 2, j * P:(j + 1) * P], Wends[:, :], start=True, stop=True)
                last.then_inc(s_rows, 1)
            pe.wait_ge(s_rowsd, NC)
            pe.wait_ge(s_rowsa, NC - 1)
            for side in range(2):
                pe.wait_ge(s_endsf, side + 1)
                for h in range(2):
                    if side:
                        pe.wait_ge(s_endsTc, h + 1)
                    for t in range(4):
                        first = (4 * h + t) * TC
                        last = nc.tensor.transpose(ps_pre[h][0:TC, t * P:(t + 1) * P], ends_f[side][:, first:first + TC], ident[:, :])
                    last.then_inc(s_endsT, 1)
            pe.wait_ge(s_reach, 1)
            nc.tensor.matmul(ps_win[0:1, 0:1], reach[:, 3:4], ones[:, 0:1], start=True, stop=True).then_inc(s_far, 1)
            pe.wait_ge(s_flag, 1)
            fast = pe.value_load(flag[0:1, 0:1], min_val=0, max_val=1)

            def program(windows):
                sides = (SRC,) if windows else (SRC, DST)
                pe.sem_inc(s_B, R)
                pe.sem_inc(s_B1, R)
                pe.sem_inc(s_T, R)

                def ea_T(n, s, g):
                    loads = s * (GS // R) + g // R + 1
                    if isinstance(s, int) and s == NS - 1:
                        loads += g // R + 1
                    pe.wait_ge(s_ea[g % R], 16 * loads)
                    if windows and g == 0:
                        pe.wait_ge(s_win_in, 16 * (s + 1))
                    pe.nop(nofuse=True)
                    nc.tensor.transpose(
                        ps_eaT[0:G * FE, 0:P],
                        ea_in[g % R][:, :, :].rearrange("p c f -> p (c f)"), ident[:, :]).then_inc(s_T, 1)

                mine, depth = plan(windows)

                def pre(n, s, g):
                    pe.wait_ge(s_Tc, n + 1)
                    if windows:
                        pe.wait_ge(s_prep, n + 1)
                    last = nc.tensor.matmul(ps_pre[g % 2][:, :], eaT[:, g % 2, :],
                                            Cblk[:, :, :].rearrange("k c f -> k (c f)"), start=True, stop=not windows)
                    by_pe = g not in mine
                    if windows:
                        for c in range(G):
                            last = nc.tensor.matmul(ps_pre[g % 2][:, c * 2 * HID:(c + 1) * 2 * HID], in_winT[:, g % R, c, :],
                                                    win_rows[:, ds(s % 2, 1), :].rearrange("p a f -> p (a f)"),
                                                    start=False, stop=c == G - 1 and not by_pe)
                    if by_pe:
                        pe.wait_ge(s_xgc, s * len(BY_PE) + BY_PE.index(g) + 1)
                        for c in range(G):
                            last = nc.tensor.matmul(ps_pre[g % 2][:, c * 2 * HID:(c + 1) * 2 * HID], xs[:, c * P:(c + 1) * P],
                                                    Wsrc[:, :], start=False, stop=c == G - 1)
                    last.then_inc(s_pre, 1)

                def feature_gather(s, g, half, made, used, product):
                    turn = s * len(BY_PE) + BY_PE.index(g)
                    for j in range(half * HALF, NB if half else HALF):
                        pe.wait_ge(made, turn * NB + j + 1)
                        last = product(BY_PE.index(g), j)
                    if half:
                        last.then_inc(used, 1)

                def ahead(s, g, made, used, product):
                    if windows:
                        for half in range(2):
                            if g + 3 - half in BY_PE:
                                feature_gather(s, g + 3 - half, half, made, used, product)

                def columns(turn, j):
                    return nc.tensor.matmul(ps_dd[DST][0][0:XW, :], xparts[:, j, :], one_of[:, j, :], start=j == 0, stop=j == NB - 1)

                def rows(turn, j):
                    for c in range(G):
                        last = nc.tensor.matmul(ps_dd[DST][turn][:, c * XW:(c + 1) * XW], one_of[:, j, c * P:(c + 1) * P], xparts[:, j, :],
                                                start=j == 0 and c == 0, stop=j == NB - 1 and c == G - 1)
                    return last

                def use(n, s, g):
                    pe.wait_ge(s_hid, n + 1)
                    pe.wait_ge(s_prep, n + 1)
                    if windows:
                        if g == 0:
                            pe.wait_ge(s_win_free, s + 1)
                        for c in range(G):
                            nc.tensor.matmul(ps_win[0:HW, 0:P], hid[:, g % 2, c, 0:HW], in_win[:, g % R, c, :],
                                             start=g == 0 and c == 0, stop=g == GS - 1 and c == G - 1)
                    for side in sides:
                        for c in range(G):
                            h0 = HW * (1 - side)
                            last = nc.tensor.matmul(ps_dd[side][g % 2][:, c * HW:(c + 1) * HW], same[side][:, g % R, c, :],
                                                    hid[:, g % 2, c, h0:h0 + HW], start=True, stop=True)
                    last.then_inc(s_B, 1)

                if windows:
                    pe.wait_ge(s_xp, 1)
                    pe.sem_inc(s_xg, 1)
                    pe.sem_inc(s_xg1, 1)
                ea_T(0, 0, 0)
                pre(0, 0, 0)
                ea_T(1, 0, 1)

                def step(s, g):
                    n = s * GS + g
                    end = isinstance(s, int) and s == NS - 1
                    if g + 1 < GS:
                        pre(n + 1, s, g + 1)
                    elif not end:
                        pre(n + 1, s + 1, 0)
                    if g + 2 < GS:
                        ea_T(n + 2, s, g + 2)
                    elif not end:
                        ea_T(n + 2, s + 1, g + 2 - GS)
                    use(n, s, g)
                    ahead(s, g, s_one, s_xg, columns)

                with pe.Fori(0, NS - 2) as s:
                    for g in range(GS):
                        step(s, g)
                for s in (NS - 2, NS - 1):
                    for g in range(GS):
                        step(s, g)

                pe.wait_ge(s_psum, 1)
                for t in range(NC + 3):
                    if t < NC:
                        j0, nj = CHUNKS[t]
                        for j in range(nj):
                            last = nc.tensor.transpose(ps_pre[t % 2][0:HW, j * P:(j + 1) * P], parts[:, 0, j0 + j, :], ident[:, :])
                        last.then_inc(s_n[0], 1)
                    if 1 <= t <= NC:
                        q = t - 1
                        w = CHUNKS[q][1] * P
                        pe.wait_ge(s_n[1], q + 1)
                        nc.tensor.matmul(ps_dd[0][q % 2][0:HID, 0:w], Wf2b[:, :], hT[:, q % 2, 0:w], start=True, stop=True).then_inc(s_n[2], 1)
                    if 2 <= t <= NC + 1:
                        q = t - 2
                        w = CHUNKS[q][1] * P
                        pe.wait_ge(s_n[3], q + 1)
                        nc.tensor.matmul(ps_dd[1][q % 2][0:HID, 0:w], Wn1s[:, :], fT[:, q % 2, 0:w], start=True, stop=True).then_inc(s_n[4], 1)
                    if t >= 3:
                        q = t - 3
                        pe.wait_ge(s_n[5], q + 1)
                        if q >= 2:
                            pe.wait_ge(s_n[7], q - 1)
                        for j in range(CHUNKS[q][1]):
                            last = nc.tensor.matmul((ps_eaT, ps_win)[q % 2][:, j * F:(j + 1) * F], uT[:, q % 2, j * P:(j + 1) * P],
                                                    Wn2b[:, :], start=True, stop=True)
                        last.then_inc(s_n[6], 1)

                def use1(n, s, g):
                    pe.wait_ge(s_prep1, n + 1)
                    if windows and g == 0:
                        pe.wait_ge(s_win1_free, s + 1)
                    if g not in mine:
                        turn = BY_PE.index(g)
                        pe.wait_ge(s_xg1c, s * len(BY_PE) + turn + 1)
                        for c in range(G):
                            last = nc.tensor.matmul(ps_dd[SRC][1][0:XW + 1, 0:P], xg[:, c, :], in_win_b[:, turn, c, :],
                                                    start=turn == 0 and c == 0, stop=turn == len(BY_PE) - 1 and c == G - 1)
                        last.then_inc(s_B1, 1)
                        return
                    o = mine.index(g)
                    for c in range(G):
                        pe.wait_ge(s_got1[o % depth][c], 16 * (s * (len(mine) // depth) + o // depth + 1))
                    for c in range(G):
                        if windows:
                            last = nc.tensor.matmul(ps_win[0:SW, 0:P], got1[:, o % depth, c, :], in_win[:, g % R, c, :],
                                                    start=o == 0 and c == 0, stop=g == mine[-1] and c == G - 1)
                        else:
                            last = nc.tensor.matmul(ps_dd[DST][g % 2][:, c * SW:(c + 1) * SW], same[DST][:, g % R, c, :],
                                                    got1[:, o % depth, c, :], start=True, stop=True)
                    last.then_inc(s_B1, 1)

                if windows:
                    pe.wait_ge(s_xp, 2)
                pe.wait_ge(s_n[7], NC)
                with pe.Fori(0, NS) as s:
                    for g in range(GS):
                        if not windows:
                            pe.wait_ge(s_sums1, s * GS + g + 1)
                        use1(s * GS + g, s, g)
                        ahead(s, g, s_one1, s_xg1, rows)
                if windows:
                    pe.wait_ge(s_win1_free, NS + 1)
                    win_cols = nei_win_sum.rearrange("f (p j) -> f j p", j=NB)
                    part_cols = nei_part_sum.rearrange("f (p j) -> f j p", j=NB)
                    for h, (j0, nj) in enumerate(((0, 15), (15, 10))):
                        for j in range(nj):
                            at = ps_pre[h][:, j * SW:(j + 1) * SW]
                            nc.tensor.matmul(at, win_cols[:, j0 + j, :], ident[0:SW, 0:SW], start=True, stop=False)
                            last = nc.tensor.matmul(at, part_cols[:, j0 + j, :], fold[:, :], start=False, stop=True)
                        last.then_inc(s_m[0], 1)
                pe.wait_ge(s_m[2], 1)

                def cat_T(q):
                    j0, nj = CHUNKS[q]
                    for j in range(nj):
                        last = nc.tensor.transpose(ps_pre[q % 2][0:2 * F, j * P:(j + 1) * P], cat[:, j0 + j, :], ident[:, :])
                    last.then_inc(s_m[3], 1)

                cat_T(0)
                for q, (j0, nj) in enumerate(CHUNKS):
                    if q + 1 < NC:
                        cat_T(q + 1)
                    pe.wait_ge(s_m[4], q + 1)
                    for j in range(j0, j0 + nj):
                        last = nc.tensor.matmul(ps_dd[1][j // 16][:, j % 16 * F:(j % 16 + 1) * F],
                                                nT[:, q % 2, (j - j0) * P:(j - j0 + 1) * P], Wb[:, :], start=True, stop=True)
                    if j0 + nj in (16, NB):
                        last.then_inc(s_m[5], 1)

            with pe.If(fast == 1):
                program(True)
            with pe.Else():
                program(False)


_INS = ['x', 'src', 'dst', 'edge_attr_16', 'L0_gnn_Wf1', 'L0_gnn_bf1', 'L0_gnn_Wf2', 'L0_gnn_bf2', 'L0_gnn_Wn1',
        'L0_gnn_bn1', 'L0_gnn_Wn2', 'L0_gnn_bn2', 'L1_gnn_W', 'L1_gnn_b']
_OUTS = [((N, F), 'float32')]


def kernel(**inputs):
    import numpy as _np
    import concourse.bacc as _bacc
    from concourse import mybir as _mybir
    from concourse.bass_utils import run_bass_kernel_spmd as _run

    nc = _bacc.Bacc("TRN2", target_bir_lowering=False, num_devices=1)
    arrays, args = {}, []
    for name in _INS:
        a = _np.ascontiguousarray(inputs[name])
        arrays[f"in_{name}_dram"] = a
        args.append(nc.dram_tensor(f"in_{name}_dram", a.shape, _mybir.dt.from_np(a.dtype), kind="ExternalInput").ap())
    for i, (shape, dtype) in enumerate(_OUTS):
        dt = _mybir.dt.from_np(_np.dtype(dtype))
        args.append(nc.dram_tensor(f"out_{i}_dram", shape, dt, kind="ExternalOutput").ap())
    build(nc, *args)
    r = _run(nc, [arrays], core_ids=[0])
    got = tuple(r.results[0][f"out_{i}_dram"] for i in range(len(_OUTS)))
    return got[0]
```

```python
import concourse.bass as bass
from concourse import mybir
from contextlib import ExitStack

P = 128
N, F = 3125, 32
E, FE = 103125, 16
HID = 64
NB = 25
NP = NB * P
NPS = NP + P
PAD_NODE = N
TRASH = N + 1
CHUNKS = [(j, min(4, NB - j)) for j in range(0, NB, 4)]
HALVES = [(0, 12), (12, 13)]
G = 4
GS = 6
CS = G * GS
ES = CS * P
NS = -(-E // ES)
NG = NS * GS
EP = NS * ES
HW = HID + 1
SW = F + 1
R = 3
PARTS = 3
XW = PARTS * F
BY_PE = (3, 4, 5)
WIDE = len(BY_PE) * G * P
SHARED = 2
WIDE1 = WIDE - SHARED * P
HOT = 12
PIECES = {2: range(0, 5), 3: range(5, 10), 4: range(10, 15), 5: range(15, 20), 0: range(20, NB)}
EARLY = (2, 3, 4, 5)
HOT_PIECES = {(g - 1) % GS: blocks for g, blocks in PIECES.items()}
HOT_EARLY = tuple(range(1, GS))
TC = 102
EPS = 1e-5
FULLX = N // NB
ELAST = E - (NS - 1) * ES
FULLE, RESTE = ELAST // CS, ELAST % CS
assert NB % HOT == 1
assert NS % 2 == 0
assert TRASH + P <= NPS and FULLX * NB == N and NS * CS % TC == 0


def build(nc, x, src, dst, ea, Wf1, bf1, Wf2, bf2, Wn1, bn1, Wn2, bn2, W, b, out):
    fp32, i32, u32 = mybir.dt.float32, mybir.dt.int32, mybir.dt.uint32
    u16, bf16 = mybir.dt.uint16, mybir.dt.bfloat16
    ALU, ACT, AX = mybir.AluOpType, mybir.ActivationFunctionType, mybir.AxisListType.X
    ds = bass.ds
    SRC, DST = 0, 1
    ctx = ExitStack()
    with ctx:
        def sb(name, shape, dt=fp32):
            return ctx.enter_context(nc.sbuf_tensor(name, shape, dt))

        def pb(name, shape):
            return ctx.enter_context(nc.psum_tensor(name, shape, fp32))

        def sem(name):
            return ctx.enter_context(nc.semaphore(name))

        ends_list = [nc.dram_tensor(f"ends_list{i}", (EP,), u16).ap() for i in range(2)]
        row_table = [nc.dram_tensor(f"row_table{i}", (NP, 2 * HID), fp32).ap() for i in range(2)]
        x1_table = nc.dram_tensor("x1_table", (NP, F), fp32).ap()
        hid_sum = [nc.dram_tensor(f"hid_sum{i}", (NPS, HW), fp32).ap() for i in range(G)]
        nei_sum = [nc.dram_tensor(f"nei_sum{i}", (NPS, SW), fp32).ap() for i in range(G)]

        xn = sb("xn", [P, NB, F])
        xparts = sb("xparts", [P, NB, XW], bf16)
        node_no = sb("node_no", [P, NB])
        node_i = sb("node_i", [P, NB], i32)
        total = xparts[:, :, :].rearrange("p j f -> p (j f)").bitcast(fp32)[:, 0:NB * SW].rearrange("p (j f) -> p j f", j=NB)
        x1 = sb("x1", [P, NB, F])
        y = sb("y", [P, NB, F])
        centred = sb("centred", [P, NB, F])
        stat = sb("stat", [P, 4, NB])
        shared = sb("shared", [P, max(G * NB * HW, NB * 4 * HID)])
        tables = shared[:, 0:NB * 4 * HID].rearrange("p (j f) -> p j f", j=NB)
        parts = shared[:, 0:G * NB * HW].rearrange("p (t j f) -> p t j f", t=G, j=NB)
        hid_win_sum = sb("hid_win_sum", [HW, NP])
        nei_win_sum = shared[0:SW, 0:NP]
        *apart, earlier = [shared[:, NP + i * G * P:NP + (i + 1) * G * P].rearrange("p (c q) -> p c q", c=G) for i in range(5)]
        Wends = sb("Wends", [F + 1, 4 * HID])
        Wsrc = sb("Wsrc", [XW, 2 * HID])
        Wsrc_parts = sb("Wsrc_parts", [XW, PARTS, 2 * HID], bf16)
        Cblk = sb("Cblk", [G * FE, G, 2 * HID])
        Wf2b = sb("Wf2b", [HW, HID])
        Wn1s = sb("Wn1s", [HID, HID])
        W2T = sb("W2T", [HID, HW])
        W21 = sb("W21", [HW, HID])
        bn1s = sb("bn1s", [HID, 1])
        Wn2b = sb("Wn2b", [HID + 1, F])
        Wself = sb("Wself", [F + 1, F])
        Wnei = sb("Wnei", [SW, SW])
        eps = sb("eps", [P, 1])
        warm = sb("warm", [P, 1])
        row_i = sb("row_i", [P, P], i32)
        col_i = sb("col_i", [P, 1], i32)
        row_no = sb("row_no", [P, P])
        col_no = sb("col_no", [P, 1])
        trash = sb("trash", [P, 1])
        below = sb("below", [P, P])
        ident = sb("ident", [P, P])
        ones = sb("ones", [P, 1])
        zrow = sb("zrow", [P, (NB + 1) * HW])
        ends = [sb(f"ends{i}", [P, NS, CS], i32) for i in range(2)]
        base_in = sb("base_in", [P, NS], i32)
        base_i = sb("base_i", [P, NS], i32)
        base = sb("base", [P, NS])
        base_p = sb("base_p", [P, NS])
        local = sb("local", [P, NS, CS])
        ends_f = [sb(f"ends_f{i}", [P, NS * CS]) for i in range(2)]
        xs_room = sb("xs_room", [P, max(WIDE, 2 * EP // TC)], bf16)
        xs = xs_room[0:XW, 0:WIDE]
        ends_T = [xs_room[0:TC, :].bitcast(u16)[:, i * EP // TC:(i + 1) * EP // TC].rearrange("r (t p) -> r t p", p=P)
                  for i in range(2)]
        reach = sb("reach", [P, 4])
        flag = sb("flag", [1, 1], i32)
        ends_bc = [sb(f"ends_bc{i}", [P, 2, ES], u16) for i in range(2)]
        ea_in = [sb(f"ea_in{r}", [P, G, FE]) for r in range(R)]
        win_rows = sb("win_rows", [P, 2, 2 * HID])
        win_parts = sb("win_parts", [P, 2, PARTS, 2 * HID], bf16)
        rest = sb("rest", [P, 2 * HID])
        get_idx = [[sb(f"get_idx{i}_{r}", [P, G], u32) for r in range(R + 1)] for i in range(2)]
        put_idx = [[sb(f"put_idx{i}_{r}", [P, G], u32) for r in range(GS)] for i in range(2)]
        one_of = sb("one_of", [P, HOT + 1, WIDE], bf16)
        no_hots = one_of[:, :, :].rearrange("p j e -> p (j e)").bitcast(fp32)

        def ring(at, depth, width):
            return no_hots[:, at:at + depth * G * width].rearrange("p (r c f) -> p r c f", r=depth, c=G)

        got = [sb("got_src", [P, R, G, 2 * HID])[:, :, :, :], ring(0, R, 2 * HID)]
        got1 = sb("nei_rows", [P, R + 1, G, SW])
        xg = sb("xg", [P, WIDE1 // P, XW + 1], bf16)
        in_win_b = sb("in_win_b", [P, len(BY_PE), G, P], bf16)
        trash_shift = [sb(f"trash_shift{i}", [P, NS, CS]) for i in range(2)]
        base_before = sb("base_before", [P, NS + 1], i32)
        same = [sb("same_src", [P, R, G, P])[:, :, :, :], ring(R * G * 2 * HID, R, P)]
        dup = sb("dup", [P, G])
        shift = sb("shift", [P, G])
        in_win = sb("in_win", [P, R, G, P])
        in_winT = sb("in_winT", [P, R, G, P], bf16)
        win_copy = sb("win_copy", [P, HW])
        eaT = sb("eaT", [G * FE, R, P])
        pre_sum = sb("pre_sum", [P, 2, G * 2 * HID])
        hid = sb("hid", [P, 2, G, 2 * HW])
        sums = [sb("sums_src", [P, 2, G, HW])[:, :, :, :], ring(R * G * (2 * HID + P), 2, HW)]
        spare = [ends_bc[i][:, :, :].rearrange("p a e -> p (a e)").bitcast(fp32) for i in range(2)]

        def two(room, rows, at):
            return room[0:rows, at:at + 8 * P].rearrange("k (a n) -> k a n", a=2)

        nT, uT = two(spare[0], SW, 0), two(spare[0], HID + 1, 8 * P)
        xT, hT = two(spare[1], F + 1, 0), two(spare[1], HW, 8 * P)
        def x1T(windows):
            return xT if windows else nT

        squares = zrow[:, 0:NB * F].rearrange("p (j f) -> p j f", j=NB)
        x1W = xn

        ps_pre = [pb(f"ps_pre{i}", [P, 512]) for i in range(2)]
        ps_dd = [[pb(f"ps_dd{i}_{j}", [P, 512]) for j in range(2)] for i in range(2)]
        ps_more = pb("ps_more", [P, 512])
        ps_win = pb("ps_win", [P, 512])
        ps_src = ps_dd[DST] + [ps_more]
        ps_src1 = (ps_src, ps_pre + ps_dd[SRC][0:1])
        def hot_slot(j):
            return j % HOT if j < NB - 1 else HOT

        EA_T = 512 - P

        s_w = sem("weights_in")
        s_we = sem("first_weights_in")
        s_x = sem("x_in")
        s_ends = sem("ends_in")
        s_iota = sem("iotas_made")
        s_zero = sem("zeros_made")
        s_eps = sem("eps_made")
        s_const = sem("constants_made")
        s_chain = sem("vector_chain")
        s_xT = sem("xT_made")
        s_xTc = sem("xT_copied")
        s_rows = sem("rows_made")
        s_rowsd = sem("rows_copied_by_dve")
        s_rowsa = sem("rows_copied_by_act")
        s_endsf = sem("ends_as_float")
        s_endsT = sem("ends_transposed")
        s_endsTc = sem("ends_T_copied")
        s_list = sem("ends_lists_written")
        s_xp = sem("x_parts_ready")
        s_tab = [sem(f"row_table_written{i}") for i in range(2)]
        s_base = sem("bases_ready")
        s_far = sem("reach_counted")
        s_reach = sem("reach_made")
        s_flag = sem("flag_made")
        s_ea = [sem(f"ea_landed{r}") for r in range(R)]
        s_win_in = sem("win_rows_landed")
        s_split = sem("split_chain")
        s_winp = sem("win_parts_ready")
        s_Wp = sem("Wsrc_parts_ready")
        s_bc = [sem(f"ends_bc_landed{i}") for i in range(2)]
        s_idx = sem("get_idx_ready")
        s_got = [[[sem(f"got{i}_{r}_{c}") for c in range(G)] for r in range(R)] for i in range(2)]
        s_link = sem("prep_chain")
        s_winT = sem("window_T_ready")
        s_prep = sem("prep_ready")
        s_T = sem("eaT_made")
        s_Tc = sem("eaT_copied")
        s_pre = sem("pre_made")
        s_a = sem("add_chain")
        s_add = sem("pre_summed")
        s_apart = sem("distances_made")
        s_mask = sem("masks_made")
        s_apart1 = sem("l1_distances_made")
        s_mask1 = sem("l1_masks_made")
        s_one = sem("one_hots_made")
        s_xg = sem("features_gathered")
        s_xgc = sem("features_copied")
        s_one1 = sem("l1_one_hots_made")
        s_xg1 = sem("l1_features_gathered")
        s_xg1c = sem("l1_features_copied")
        s_hid = sem("hid_ready")
        s_B = sem("hid_used")
        s_sums = sem("sums_ready")
        s_sums_free = sem("sums_free")
        s_put = [sem(f"hid_scattered{c}") for c in range(G)]
        s_winc = sem("window_copied")
        s_winn = sem("window_turned")
        s_win_free = sem("ps_win_free")
        s_parts = [sem(f"hid_sums_in{h}") for h in range(2)]
        s_psum = sem("hid_summed")
        s_W2T = sem("Wf2_transposed")
        s_W2Tc = sem("Wf2_T_copied")
        s_W21 = sem("W21_made")
        s_W21c = sem("W21_copied")
        s_sumT = sem("hid_sums_transposed")
        s_hT = sem("hT_ready")
        s_u = sem("first_products_made")
        s_uT = sem("uT_ready")
        s_second = sem("second_products_made")
        s_y0 = sem("update_added")
        s_sq = sem("sqrt_asked")
        s_sqd = sem("sqrt_done")
        s_x1T = sem("x1_transposed")
        s_x1Tc = sem("x1_T_copied")
        s_x1W = sem("x1_products_made")
        s_x1Wc = sem("x1_products_copied")
        s_x1 = sem("x1_ready")
        s_x1t = sem("x1_table_written")
        s_idx1 = sem("l1_get_idx_ready")
        s_got1 = [[sem(f"l1_got_{r}_{c}") for c in range(G)] for r in range(R + 1)]
        s_link1 = sem("l1_prep_chain")
        s_prep1 = sem("l1_prep_ready")
        s_B1 = sem("l1_rows_used")
        s_sums1 = sem("l1_sums_ready")
        s_sums1_free = sem("l1_sums_free")
        s_put1 = [sem(f"l1_scattered{c}") for c in range(G)]
        s_win1c = sem("l1_window_copied")
        s_win1n = sem("l1_window_turned")
        s_win1_free = sem("l1_ps_win_free")
        s_parts1 = sem("l1_sums_in")
        s_total = sem("neighbour_sums_ready")
        s_totalT = sem("neighbour_sums_transposed")
        s_totalTc = sem("neighbour_sums_T_copied")
        s_nei = sem("neighbour_products_made")
        s_y = sem("result_ready")
        s_out = sem("out_written")

        W_DMAS = 2 * G + 2 + 1 + 1 + 2 + 3 + 2 * PARTS
        NC = len(CHUNKS)
        ENDS_AT = 3

        def plan(windows):
            mine = [g for g in range(GS) if not (windows and g in BY_PE)]
            return mine, R

        def bc_rows(side, s):
            return ends_list[side][ds(s * ES, ES)].rearrange("(a n) -> a n", a=1).to_broadcast([P, ES])

        block = ctx.enter_context(nc.Block())

        @block.sync
        def _(sp):
            sp.wait_ge(s_zero, 1)
            sp.dma_start(xn[0:FULLX, :, :], x.rearrange("(p j) f -> p j f", j=NB)).then_inc(s_x, 16)
            cut0 = (NS - 1) * ES
            cut1 = cut0 + FULLE * CS
            for side, e in ((DST, dst), (SRC, src)):
                sp.dma_start(ends[side][:, 0:NS - 1, :], e[0:cut0].rearrange("(s p c) -> p s c", p=P, c=CS)).then_inc(s_ends, 16)
                sp.dma_start(ends[side][0:FULLE, NS - 1, :], e[cut0:cut1].rearrange("(p c) -> p c", c=CS)).then_inc(s_ends, 16)
                sp.dma_start(ends[side][FULLE:FULLE + 1, NS - 1, 0:RESTE], e[cut1:E].rearrange("(p c) -> p c", p=1)).then_inc(s_ends, 16)
            with nc.allow_non_contiguous_dma(reason="one base per supertile"):
                sp.dma_start(base_in[:, 0:NS - 1], dst[0:cut0].rearrange("(s e) -> e s", e=ES)[0:1, :]
                             .to_broadcast([P, NS - 1])).then_inc(s_ends, 16)
                sp.dma_start(base_in[:, NS - 1:NS], dst[cut0:cut0 + 1].rearrange("(a n) -> a n", a=1)
                             .to_broadcast([P, 1])).then_inc(s_ends, 16)
            def write_rows(side, j0, j1):
                lo = 2 * HID * (1 - side)
                sp.dma_start(row_table[side].rearrange("(p j) f -> p j f", j=NB)[:, j0:j1, :],
                             tables[:, j0:j1, lo:lo + 2 * HID]).then_inc(s_tab[side], 16)

            def write_list(side):
                sp.wait_ge(s_endsTc, 2 * (side + 1))
                sp.dma_start(ends_list[side].rearrange("(t r p) -> r t p", r=TC, p=P), ends_T[side][:, :, :]).then_inc(s_list, 16)

            half = CHUNKS[NC // 2][0]
            sp.wait_ge(s_rowsd, NC // 2)
            sp.wait_ge(s_rowsa, NC // 2)
            for side in (DST, SRC):
                write_rows(side, 0, half)
            write_list(SRC)
            write_list(DST)
            sp.wait_ge(s_rowsd, NC)
            sp.wait_ge(s_rowsa, NC - 1)
            for side in (DST, SRC):
                write_rows(side, half, NB)
            sp.wait_ge(s_list, 32)
            sp.wait_ge(s_flag, 1)
            fast = sp.value_load(flag[0:1, 0:1], min_val=0, max_val=1)

            def program(windows):
                if windows:
                    sp.wait_ge(s_base, 1)

                def load_ea(n, s, g):
                    sp.wait_ge(s_T, n + 1)
                    cols = slice(g * G, (g + 1) * G)
                    if isinstance(s, int) and s == NS - 1:
                        first, rest = s * ES, min(G, RESTE - g * G)
                        sp.dma_start(ea_in[g % R][0:FULLE, :, :],
                                     ea[first:first + FULLE * CS, :].rearrange("(p c) f -> p c f", c=CS)[:, cols, :]).then_inc(s_ea[g % R], 16)
                        first += FULLE * CS + g * G
                        sp.dma_start(ea_in[g % R][FULLE:FULLE + 1, 0:rest, :],
                                     ea[first:first + rest, :].rearrange("(p c) f -> p c f", p=1)).then_inc(s_ea[g % R], 16)
                    else:
                        sp.dma_start(ea_in[g % R][:, :, :],
                                     ea[ds(s * ES, ES), :].rearrange("(p c) f -> p c f", c=CS)[:, cols, :]).then_inc(s_ea[g % R], 16)

                def load_window(s):
                    if windows:
                        first = sp.value_load(base_i[0:1, ds(s, 1)], min_val=0, max_val=NP - P)
                        sp.dma_start(win_rows[:, ds(s % 2, 1), :].rearrange("p a f -> p (a f)"),
                                     row_table[DST][ds(first, P), :]).then_inc(s_win_in, 16)

                def load_ends(s):
                    for side in range(2):
                        sp.dma_start(ends_bc[side][:, ds(s % 2, 1), :].rearrange("p a e -> p (a e)"),
                                     bc_rows(side, s)).then_inc(s_bc[side], 16)

                def supertile(s, first=False):
                    for g in range(GS):
                        load_ea(s * GS + g, s, g)
                        if g == 3 and not (isinstance(s, int) and s == NS - 1):
                            sp.wait_ge(s_pre, s * GS + 1)
                            sp.wait_ge(s_prep, s * GS + 1)
                            load_window(s + 1)
                            load_ends(s + 1)

                load_ends(0)
                if windows:
                    sp.wait_ge(s_tab[DST], 32)
                load_window(0)
                with sp.Fori(0, NS - 1) as s:
                    supertile(s)
                supertile(NS - 1)
                puts = NG if windows else 2 * NG
                for h, (j0, nj) in enumerate(HALVES):
                    for t in range(G):
                        sp.wait_ge(s_put[t], 16 * (1 + puts))
                        sp.dma_start(parts[:, t, j0:j0 + nj, :],
                                     hid_sum[t][0:NP, :].rearrange("(p j) f -> p j f", j=NB)[:, j0:j0 + nj, :]).then_inc(s_parts[h], 16)
                sp.wait_ge(s_x1, 1)
                sp.dma_start(x1_table.rearrange("(p j) f -> p j f", j=NB), x1[:, :, :]).then_inc(s_x1t, 16)
                again = SRC if windows else DST
                sp.wait_ge(s_y0, NC)
                if windows:
                    sp.wait_ge(s_one, NS * NB)
                sp.dma_start(ends_bc[again][:, 0, :], bc_rows(again, 0)).then_inc(s_bc[again], 16)
                with sp.Fori(1, NS) as s:
                    if windows:
                        sp.wait_ge(s_one1, (s - 1) * NB + 1)
                    else:
                        sp.wait_ge(s_mask1, (s - 1) * GS + 1)
                    sp.dma_start(ends_bc[again][:, ds(s % 2, 1), :].rearrange("p a e -> p (a e)"), bc_rows(again, s)).then_inc(s_bc[again], 16)
                if not windows:
                    for t in range(G):
                        sp.wait_ge(s_put1[t], 16 * (1 + NG))
                        sp.dma_start(parts[:, t, :, 0:SW], nei_sum[t][0:NP, :].rearrange("(p j) f -> p j f", j=NB)).then_inc(s_parts1, 16)
                sp.wait_ge(s_x1t, 16)
                sp.wait_ge(s_y, 1)
                sp.dma_start(out.rearrange("(p j) f -> p j f", j=NB), y[0:FULLX, :, :]).then_inc(s_out, 16)
                sp.wait_ge(s_out, 16)

            with sp.If(fast == 1):
                program(True)
            with sp.Else():
                program(False)

        @block.gpsimd
        def _(pool):
            nc.gpsimd.iota(row_i[:, :], pattern=[[1, P]], base=0, channel_multiplier=0).then_inc(s_iota, 1)
            nc.gpsimd.iota(col_i[:, :], pattern=[[0, 1]], base=0, channel_multiplier=1).then_inc(s_iota, 1)
            nc.gpsimd.iota(node_i[:, :], pattern=[[1, NB]], base=0, channel_multiplier=NB).then_inc(s_iota, 1)
            pool.wait_ge(s_zero, 1)
            for t in range(G):
                pool.dma_start(hid_sum[t].rearrange("(p j) f -> p (j f)", p=P), zrow[:, 0:NPS // P * HW]).then_inc(s_put[t], 16)
            pool.wait_ge(s_tab[SRC], 32)
            for t in range(G):
                pool.wait_ge(s_put[t], 16)
            pool.wait_ge(s_flag, 1)
            fast = pool.value_load(flag[0:1, 0:1], min_val=0, max_val=1)

            def program(windows):
                sides = (SRC,) if windows else (SRC, DST)
                if not windows:
                    pool.wait_ge(s_tab[DST], 32)
                    for t in range(G):
                        pool.dma_start(nei_sum[t].rearrange("(p j) f -> p (j f)", p=P), zrow[:, 0:NPS // P * SW]).then_inc(s_put1[t], 16)
                    for t in range(G):
                        pool.wait_ge(s_put1[t], 16)

                mine, depth = plan(windows)
                k_mine = len(mine)

                def gather(m, o, columns=range(G)):
                    pool.wait_ge(s_idx, m + 1)
                    pool.nop(nofuse=True)
                    for side in sides:
                        for c in columns:
                            pool.indirect_dma_start(
                                out=got[side][:, o % depth, c, :], out_offset=None, in_=row_table[side],
                                in_offset=bass.IndirectOffsetOnAxis(ap=get_idx[side][o % depth][:, c:c + 1], axis=0))\
                                .then_inc(s_got[side][o % depth][c], 16)

                def scatter(n, g):
                    pool.wait_ge(s_sums, n + 1)
                    pool.wait_ge(s_prep, n + 1)
                    for j, side in enumerate(sides):
                        for c in range(G):
                            pool.wait_ge(s_put[c], 16 * (len(sides) * n + j + 1))
                            nop = pool.nop(nofuse=True)
                            if j == 0 and c == G - 1:
                                nop.then_inc(s_sums_free, 1)
                            pool.indirect_dma_start(
                                out=hid_sum[c], in_=sums[side][:, g % 2, c, :], in_offset=None,
                                out_offset=bass.IndirectOffsetOnAxis(ap=put_idx[side][g][:, c:c + 1], axis=0),
                                compute_op=ALU.add).then_inc(s_put[c], 16)

                pool.sem_inc(s_sums_free, 1)
                lead = depth - 1
                halves = (range(0, G // 2), range(G // 2, G))

                def first(gather):
                    for o in range(lead):
                        gather(o, o)
                    if windows:
                        gather(lead, lead, halves[0])

                first(gather)

                def step1(s, g):
                    last = isinstance(s, int) and s == NS - 1
                    if g == 0:
                        gather1(s * (R + 1) + R - 1, R - 1, halves[1])
                        if not (isinstance(s, int) and s == 0):
                            pool.wait_ge(s_B1, R + (s - 1) * GS + R + 1)
                        gather1(s * (R + 1) + R, R, range(SHARED))
                    elif not last:
                        o = (g - 1) // 2
                        pool.wait_ge(s_B1, R + s * GS + o + 1)
                        gather1((s + 1) * (R + 1) + o, o, halves[(g - 1) % 2])

                def step(s, g, gather, scatter):
                    if windows:
                        if g == 0:
                            gather(s * k_mine + lead, lead, halves[1])
                        elif not (isinstance(s, int) and s == NS - 1):
                            o = (g - 1) // 2
                            gather((s + 1) * k_mine + o, o, halves[(g - 1) % 2])
                    elif g in mine:
                        o = mine.index(g)
                        if not (isinstance(s, int) and s == NS - 1 and o + lead >= k_mine):
                            gather(s * k_mine + o + lead, (o + lead) % k_mine)
                    if scatter:
                        scatter(s * GS + g, g)

                with pool.Fori(0, NS - 1) as s:
                    for g in range(GS):
                        step(s, g, gather, scatter)
                for g in range(GS):
                    step(NS - 1, g, gather, scatter)

                pool.wait_ge(s_x1t, 16)
                if not windows:
                    pool.sem_inc(s_sums1_free, 1)

                def gather1(m, o, columns=range(G)):
                    pool.wait_ge(s_idx1, m + 1)
                    o = o if windows else o % depth
                    pool.nop(nofuse=True)
                    for c in columns:
                        pool.indirect_dma_start(
                            out=got1[:, o, c, 0:F], out_offset=None, in_=x1_table,
                            in_offset=bass.IndirectOffsetOnAxis(ap=get_idx[SRC][o][:, c:c + 1], axis=0))\
                            .then_inc(s_got1[o][c], 16)

                def scatter1(n, g):
                    pool.wait_ge(s_sums1, n + 1 + 2)
                    pool.wait_ge(s_prep1, n + 1)
                    for c in range(G):
                        pool.wait_ge(s_put1[c], 16 * (n + 1))
                    pool.nop(nofuse=True).then_inc(s_sums1_free, 1)
                    for c in range(G):
                        pool.indirect_dma_start(
                            out=nei_sum[c], in_=sums[DST][:, g % 2, c, 0:SW], in_offset=None,
                            out_offset=bass.IndirectOffsetOnAxis(ap=put_idx[DST][g][:, c:c + 1], axis=0),
                            compute_op=ALU.add).then_inc(s_put1[c], 16)

                first(gather1)
                for g in range(GS):
                    step1(0, g) if windows else step(0, g, gather1, scatter1)
                with pool.Fori(1, NS - 1) as s:
                    for g in range(GS):
                        step1(s, g) if windows else step(s, g, gather1, scatter1)
                for g in range(GS):
                    step1(NS - 1, g) if windows else step(NS - 1, g, gather1, scatter1)

            with pool.If(fast == 1):
                program(True)
            with pool.Else():
                program(False)

        @block.scalar
        def _(act):
            act.wait_ge(s_eps, 1)
            nc.scalar.activation(warm[:, :], eps[:, :], ACT.Sqrt)

            def copy_xT(q):
                act.wait_ge(s_xT, q + 1)
                w = CHUNKS[q][1] * P
                nc.scalar.activation(xT[0:F, q % 2, 0:w], (ps_more, ps_win)[q % 2][0:F, 0:w], ACT.Copy).then_inc(s_xTc, 1)

            both = Wf1[0:2 * F, :].rearrange("(k r) f -> r k f", k=2)
            act.dma_start(Wends[0:F, 0:2 * HID].rearrange("r (k f) -> r k f", k=2), both).then_inc(s_we, 16)
            for k in range(2):
                act.dma_start(Wends[0:F, (2 + k) * HID:(3 + k) * HID], Wf1[F * (1 - k):F * (2 - k), :]).then_inc(s_we, 16)
            act.wait_ge(s_zero, 1)
            for k in range(2):
                act.dma_start(Wends[F:F + 1, k * HID:(k + 1) * HID], bf1.rearrange("(a n) -> a n", a=1)).then_inc(s_we, 16)
            def row(vector):
                return vector.rearrange("(a n) -> a n", a=1)

            C = Wf1[2 * F:2 * F + FE, :]
            weights = [(Wn1s[:, :], Wn1), (bn1s[:, :], bn1.rearrange("(n a) -> n a", a=1)),
                       (Wf2b[0:HID, :], Wf2), (Wf2b[HID:HW, :], row(bf2)), (Wn2b[0:HID, :], Wn2), (Wn2b[HID:HID + 1, :], row(bn2)),
                       (Wself[0:F, :], W[0:F, :]), (Wself[F:F + 1, :], row(b)), (Wnei[0:F, 0:F], W[F:2 * F, :])]
            for k in range(2):
                weights += [(Cblk[c * FE:(c + 1) * FE, c, k * HID:(k + 1) * HID], C) for c in range(G)]
                weights += [(Wsrc[t * F:(t + 1) * F, k * HID:(k + 1) * HID], Wf1[F * (1 - k):F * (2 - k), :])
                            for t in range(PARTS)]
            assert len(weights) == W_DMAS
            copy_xT(0)
            for q, (j0, nj) in enumerate(CHUNKS):
                if q + 1 < NC:
                    copy_xT(q + 1)
                for to, weight in weights[4 * q:4 * q + 4]:
                    act.dma_start(to, weight).then_inc(s_w, 16)
                if nj > 2:
                    act.wait_ge(s_rows, q + 1)
                    nc.scalar.activation(tables[:, j0 + 2:j0 + nj, :],
                                         (ps_pre[1], ps_dd[SRC][1])[q % 2][:, 0:(nj - 2) * 4 * HID]
                                         .rearrange("p (j f) -> p j f", f=4 * HID), ACT.Copy).then_inc(s_rowsa, 1)
                if q - ENDS_AT in (SRC, DST):
                    side = q - ENDS_AT
                    for h in range(2):
                        act.wait_ge(s_endsT, 2 * side + h + 1)
                        nc.scalar.activation(ends_T[side][:, 4 * h:4 * h + 4, :],
                                             ps_dd[DST][h][0:TC, :].rearrange("r (t p) -> r t p", t=4), ACT.Copy).then_inc(s_endsTc, 1)
            act.wait_ge(s_flag, 1)
            fast = act.value_load(flag[0:1, 0:1], min_val=0, max_val=1)

            def program(windows):
                sides = (SRC,) if windows else (SRC, DST)

                def copy_eaT(n, g):
                    act.wait_ge(s_T, R + n + 1)
                    nc.scalar.activation(eaT[:, g % R, :], ps_dd[SRC][(g + 1) % 2][0:G * FE, EA_T:512], ACT.Copy).then_inc(s_Tc, 1)

                mine, depth = plan(windows)
                k_mine = len(mine)

                def relu(n, s, g):
                    if g in mine:
                        act.wait_ge(s_add, s * k_mine + mine.index(g) + 1)
                        before = pre_sum[:, g % 2, :]
                    else:
                        act.wait_ge(s_pre, n + 1)
                        before = ps_pre[g % 2][:, :]
                    nc.scalar.activation(
                        hid[:, g % 2, :, :].rearrange("p c (k f) -> p c k f", k=2)[:, :, :, 0:HID],
                        before.rearrange("p (c k f) -> p c k f", c=G, k=2), ACT.Relu).then_inc(s_hid, 1)

                def copy_xs(s):
                    act.wait_ge(s_xg, HOT + (s + 1) * NB)
                    for k in range(len(BY_PE)):
                        nc.scalar.activation(xs[:, k * G * P:(k + 1) * G * P], ps_src[k][0:XW, :], ACT.Copy).then_inc(s_xgc, 1)

                def col(side, s, g, c):
                    return ends_f[side][:, :].rearrange("p (s c) -> p s c", s=NS)[:, ds(s, 1), g * G + c:g * G + c + 1].rearrange("p a c -> p (a c)")

                def equal(jobs, n, distance, made, room=0):
                    for k, (to, scalars, others) in enumerate(jobs):
                        for c in range(G):
                            last = nc.scalar.activation(apart[room + k][:, c, :], others(c), ACT.Abs, bias=scalars(c), scale=-1.0)
                        last.then_inc(distance, 1)
                    for k, (to, scalars, others) in enumerate(jobs):
                        act.wait_ge(distance, n * len(jobs) + k + 1)
                        c = 0
                        for some in to:
                            last = nc.scalar.activation(some, apart[room + k][:, c:c + some.shape[1], :], ACT.Relu, bias=ones[:, 0:1], scale=-1.0)
                            c += some.shape[1]
                    last.then_inc(made, 1)

                def job_same(side, s, g):
                    return ((same[side][:, g % R, :, :],), lambda c: col(side, s, g, c),
                            lambda c: ends_bc[side][:, ds(s % 2, 1), (g * G + c) * P:(g * G + c + 1) * P].rearrange("p a q -> p (a q)"))

                def job_window(to, s, g):
                    return (to, lambda c: local[:, ds(s, 1), g * G + c:g * G + c + 1].rearrange("p a c -> p (a c)"),
                            lambda c: row_no[:, :])

                def masks(n, s, g):
                    act.wait_ge(s_B, n + 1)
                    for side in sides:
                        act.wait_ge(s_bc[side], 16 * (s + 1))
                    jobs = [job_same(side, s, g) for side in sides]
                    if windows:
                        jobs.append(job_window((in_win[:, g % R, :, :],), s, g))
                    equal(jobs, n, s_apart, s_mask, 2 * (g % 2))

                def copy_sums(n, g):
                    act.wait_ge(s_B, R + n + 1)
                    act.wait_ge(s_sums_free, n + 1)
                    for side in sides:
                        last = nc.scalar.activation(
                            sums[side][:, g % 2, :, :],
                            ps_dd[side][g % 2][:, 0:G * HW].rearrange("p (c f) -> p c f", c=G), ACT.Copy)
                    last.then_inc(s_sums, 1)

                for side in range(2):
                    act.wait_ge(s_tab[side], 32)
                masks(0, 0, 0)
                copy_eaT(0, 0)
                copy_eaT(1, 1)
                copy_eaT(2, 2)
                masks(1, 0, 1)

                def step(s, g):
                    n = s * GS + g
                    more = not (isinstance(s, int) and g + 2 >= GS)
                    relu(n, s, g)
                    if more:
                        masks(n + 2, s + (g + 2) // GS, (g + 2) % GS)
                    if windows and g == BY_PE[0] - 2:
                        copy_xs(s)
                    if windows and g == GS - 1:
                        act.wait_ge(s_B, R + n + 1)
                        nc.scalar.activation(win_copy[:, :], ps_win[:, 0:HW], ACT.Copy).then_inc(s_winc, 1)
                    copy_sums(n, g)
                    if not (isinstance(s, int) and g + R >= GS):
                        copy_eaT(n + R, (g + R) % GS)

                with act.Fori(0, NS - 1) as s:
                    for g in range(GS):
                        step(s, g)
                for g in range(GS):
                    step(NS - 1, g)
                act.wait_ge(s_W2T, 1)
                nc.scalar.activation(W2T[:, :], ps_more[0:HID, 0:HW], ACT.Copy).then_inc(s_W2Tc, 1)
                act.wait_ge(s_W21, 1)
                nc.scalar.activation(W21[:, :], ps_more[0:HW, 0:HID], ACT.Copy).then_inc(s_W21c, 1)
                for q, (j0, nj) in enumerate(CHUNKS):
                    w = nj * P
                    act.wait_ge(s_u, q + 1)
                    nc.scalar.activation(uT[0:HID, q % 2, 0:w], ps_dd[1][q % 2][0:HID, 0:w], ACT.Relu, bias=bn1s[:, 0:1]).then_inc(s_uT, 1)
                act.wait_ge(s_sq, 1)
                nc.scalar.activation(stat[:, 2, :], stat[:, 1, :], ACT.Sqrt, bias=eps[:, 0:1], scale=1.0 / F).then_inc(s_sqd, 1)
                for q, (j0, nj) in enumerate(CHUNKS):
                    act.wait_ge(s_x1T, q + 1)
                    nc.scalar.activation(x1T(windows)[0:F, q % 2, 0:nj * P], ps_pre[q % 2][0:F, 0:nj * P], ACT.Copy).then_inc(s_x1Tc, 1)
                for h, (j0, nj) in enumerate(HALVES):
                    act.wait_ge(s_x1W, h + 1)
                    nc.scalar.activation(x1W[:, j0:j0 + nj, :], ps_dd[SRC][h][:, 0:nj * F].rearrange("p (j f) -> p j f", j=nj),
                                         ACT.Copy).then_inc(s_x1Wc, 1)

                def masks1(n, s, g):
                    act.wait_ge(s_B1, n + 1)
                    if windows:
                        if g == BY_PE[0]:
                            to = (in_win[:, g % R, 0:SHARED, :], in_win_b[:, 0, SHARED:G, :])
                        else:
                            to = (in_win[:, g % R, :, :] if g in mine else in_win_b[:, BY_PE.index(g), :, :],)
                        equal([job_window(to, s, g)], n, s_apart1, s_mask1, g % R)
                    else:
                        act.wait_ge(s_bc[DST], 16 * (s + 1 + NS))
                        equal([job_same(DST, s, g)], n, s_apart1, s_mask1, g % R)

                def copy_sums1(n, g):
                    act.wait_ge(s_B1, R + n + 1)
                    act.wait_ge(s_sums1_free, n + 1)
                    nc.scalar.activation(
                        sums[DST][:, g % 2, :, 0:SW],
                        ps_dd[DST][g % 2][:, 0:G * SW].rearrange("p (c f) -> p c f", c=G), ACT.Copy).then_inc(s_sums1, 1)

                def copy_xg(s, parity):
                    act.wait_ge(s_xg1, HOT + (s + 1) * NB)
                    act.wait_ge(s_B1, R + s * GS + 1)
                    for k in range(len(BY_PE)):
                        n_cols = min(G, WIDE1 // P - k * G)
                        nc.scalar.activation(xg[:, k * G:k * G + n_cols, 0:XW],
                                             ps_src1[parity][k][:, 0:n_cols * XW].rearrange("p (c f) -> p c f", c=n_cols), ACT.Copy).then_inc(s_xg1c, 1)

                if not windows:
                    act.sem_inc(s_sums1, 2)
                masks1(0, 0, 0)
                masks1(1, 0, 1)

                def step1(s, parity, g):
                    n = s * GS + g
                    if windows and g == BY_PE[0] - 2:
                        copy_xg(s, parity)
                    if not windows:
                        copy_sums1(n, g)
                    if not (isinstance(s, int) and s == NS - 1 and g + 2 >= GS):
                        masks1(n + 2, s + (g + 2) // GS, (g + 2) % GS)
                    if windows and g == GS - 1:
                        act.wait_ge(s_B1, R + n + 1)
                        nc.scalar.activation(win_copy[:, 0:SW], ps_win[:, 0:SW], ACT.Copy).then_inc(s_win1c, 1)

                with act.Fori(0, NS // 2 - 1) as pair:
                    for parity in range(2):
                        for g in range(GS):
                            step1(pair * 2 + parity, parity, g)
                for s in (NS - 2, NS - 1):
                    for g in range(GS):
                        step1(s, s % 2, g)
                if not windows:
                    for q, (j0, nj) in enumerate(CHUNKS):
                        act.wait_ge(s_totalT, q + 1)
                        nc.scalar.activation(nT[:, q % 2, 0:nj * P], ps_dd[SRC][q % 2][0:SW, 0:nj * P], ACT.Copy).then_inc(s_totalTc, 1)
                act.wait_ge(s_sq, 2)
                nc.scalar.activation(stat[:, 2, :], stat[:, 1, :], ACT.Sqrt, bias=eps[:, 0:1], scale=1.0 / F).then_inc(s_sqd, 1)

            with act.If(fast == 1):
                program(True)
            with act.Else():
                program(False)

        @block.vector
        def _(dve):
            chain = [0]

            def link(ins):
                chain[0] += 1
                ins.then_inc(s_chain, 1)
                dve.wait_ge(s_chain, chain[0])

            v = nc.vector
            v.memset(eps[:, :], EPS).then_inc(s_eps, 1)
            v.memset(ends[DST][:, NS - 1, :], PAD_NODE)
            v.memset(ends[SRC][:, NS - 1, :], PAD_NODE)
            v.memset(xn[96:P, :, :], 0.0)
            v.memset(Cblk[:, :, :], 0.0)
            v.memset(Wends[F:F + 1, :], 0.0)
            v.memset(Wnei[0:F, F:SW], 0.0)
            v.memset(Wnei[F:SW, 0:F], 0.0)
            v.memset(Wnei[F:SW, F:SW], 1.0)
            v.memset(zrow[:, :], 0.0).then_inc(s_zero, 1)
            v.memset(xT[F:F + 1, :, :], 1.0)
            v.memset(ones[:, :], 1.0)
            v.memset(xg[:, :, XW:XW + 1], 1.0)
            v.memset(got1[:, :, :, F:SW], 1.0)
            for k in range(2):
                v.memset(hid[:, :, :, k * HW + HID:(k + 1) * HW], 1.0)
            dve.wait_ge(s_iota, 3)
            v.tensor_copy(row_no[:, :], row_i[:, :])
            v.tensor_copy(node_no[:, :], node_i[:, :])
            link(v.tensor_copy(col_no[:, :], col_i[:, :]))
            v.tensor_scalar(trash[:, :], col_no[:, :], float(TRASH), None, ALU.add)
            v.tensor_scalar(below[:, :], row_no[:, :], col_no[:, 0:1], None, ALU.is_lt)
            v.tensor_scalar(ident[:, :], row_no[:, :], col_no[:, 0:1], None, ALU.is_equal).then_inc(s_const, 1)
            def bases():
                link(v.tensor_scalar(base[:, :], base_in[:, :], float(NP - P), None, ALU.min))

            def distances():
                link(v.tensor_tensor(local[:, :, :], ends[DST][:, :, :],
                                     base[:, :].rearrange("p (s a) -> p s a", a=1).to_broadcast([P, NS, CS]), ALU.subtract))

            def farthest():
                flat = local[:, :, :].rearrange("p s c -> p (s c)")
                v.tensor_reduce(out=reach[:, 0:1], in_=flat, axis=AX, op=ALU.max)
                link(v.tensor_reduce(out=reach[:, 1:2], in_=flat, axis=AX, op=ALU.min))
                v.tensor_scalar(reach[:, 2:3], reach[:, 0:1], P - 0.5, None, ALU.is_gt)
                link(v.tensor_scalar(reach[:, 1:2], reach[:, 1:2], -0.5, None, ALU.is_lt))
                v.tensor_tensor(reach[:, 3:4], reach[:, 1:2], reach[:, 2:3], ALU.add).then_inc(s_reach, 1)

            def floats():
                dve.wait_ge(s_ends, 16 * 8)
                for side in range(2):
                    v.tensor_copy(ends_f[side][:, :], ends[side][:, :, :].rearrange("p s c -> p (s c)")).then_inc(s_endsf, 1)

            between = {1: floats, 2: bases, 3: distances, 4: farthest}
            for q, (j0, nj) in enumerate(CHUNKS):
                dve.wait_ge(s_rows, q + 1)
                w = min(nj, 2)
                v.tensor_copy(tables[:, j0:j0 + w, :], (ps_pre[0], ps_dd[SRC][0])[q % 2][:, 0:w * 4 * HID]
                              .rearrange("p (j f) -> p j f", f=4 * HID)).then_inc(s_rowsd, 1)
                if q in between:
                    between[q]()
            dve.wait_ge(s_far, 1)
            v.tensor_scalar(flag[:, :], ps_win[0:1, 0:1], 0.5, None, ALU.is_lt).then_inc(s_flag, 1)
            v.tensor_copy(base_i[:, :], base[:, :]).then_inc(s_base, 1)
            v.memset(base_before[:, 0:1], 0)
            v.tensor_copy(base_before[:, 1:NS + 1], base[:, :])
            v.tensor_scalar(base_p[:, :], base[:, :], col_no[:, 0:1], None, ALU.add)
            v.memset(hid_win_sum[:, :], 0.0)
            for side in range(2):
                v.tensor_scalar(trash_shift[side][:, :, :], ends[side][:, :, :], -1.0, trash[:, 0:1], ALU.mult, ALU.add)
            def split(whole, part, over, after):
                after(v.tensor_copy(part[0], whole))
                after(v.tensor_tensor(over, whole, part[0], ALU.subtract))
                after(v.tensor_copy(part[1], over))
                return v.tensor_tensor(part[2], over, part[1], ALU.subtract)

            def split_x(whole):
                return split(whole[:, :, :], [xparts[:, :, t * F:(t + 1) * F] for t in range(PARTS)], centred[:, :, :], link)

            split_x(xn).then_inc(s_xp, 1)
            dve.wait_ge(s_flag, 1)
            fast = dve.value_load(flag[0:1, 0:1], min_val=0, max_val=1)

            before = chain[0]

            def program(windows):
                chain[0] = before
                sides = (SRC,) if windows else (SRC, DST)

                mine, depth = plan(windows)
                k_mine = len(mine)

                def copy_idx(s, o, which, signal):
                    for side in which:
                        last = v.tensor_copy(get_idx[side][o % depth][:, :], col(side, s, mine[o]))
                    last.then_inc(signal, 1)

                def col(side, s, g):
                    return ends[side][:, ds(s, 1), g * G:(g + 1) * G].rearrange("p a c -> p (a c)")

                def bcast(side, s, g):
                    return ends_bc[side][:, ds(s % 2, 1), g * G * P:(g + 1) * G * P].rearrange("p a (c q) -> p (a c) q", q=P)

                def rows(small):
                    return small.rearrange("p (a q) -> p a q", a=1).to_broadcast([P, G, P])

                def cols(array, s, g):
                    return array[:, ds(s, 1), g * G:(g + 1) * G].rearrange("p a c -> p (a c)")

                def dedup(side, s, g, after):
                    after(v.tensor_tensor(earlier[:, :, :], same[side][:, g % R, :, :], rows(below[:, :]), ALU.mult))
                    after(v.tensor_reduce(out=dup[:, :], in_=earlier[:, :, :], axis=AX, op=ALU.max))
                    after(v.tensor_tensor(shift[:, :], cols(trash_shift[side], s, g), dup[:, :], ALU.mult))
                    return v.tensor_tensor(put_idx[side][g][:, :], shift[:, :], col(side, s, g), ALU.add)

                LINKS = 3 * len(sides)

                def prep(n, s, g):
                    count = [0]

                    def after(ins):
                        count[0] += 1
                        ins.then_inc(s_link, 1)
                        dve.wait_ge(s_link, n * LINKS + count[0])

                    dve.wait_ge(s_mask, n + 1)
                    for side in sides:
                        last = dedup(side, s, g, after)
                    last.then_inc(s_prep, 1)

                def window_T(n, s, g):
                    if windows:
                        dve.wait_ge(s_bc[DST], 16 * (s + 1))
                        dve.wait_ge(s_B, n + 1)
                        v.tensor_scalar(in_winT[:, g % R, :, :], bcast(DST, s, g), base_p[:, ds(s, 1)], None,
                                        ALU.is_equal).then_inc(s_winT, 1)

                def add(n, s, g):
                    o = mine.index(g)
                    dve.wait_ge(s_pre, n + 1)
                    for side in sides:
                        for c in range(G):
                            dve.wait_ge(s_got[side][o % depth][c], 16 * (s * (k_mine // depth) + o // depth + 1))
                    acc = pre_sum[:, g % 2, :]
                    ins = v.tensor_tensor(acc, ps_pre[g % 2][:, :],
                                          got[SRC][:, o % depth, :, :].rearrange("p c f -> p (c f)"), ALU.add)
                    if not windows:
                        ins.then_inc(s_a, 1)
                        dve.wait_ge(s_a, n + 1)
                        ins = v.tensor_tensor(acc, acc, got[DST][:, o % depth, :, :].rearrange("p c f -> p (c f)"), ALU.add)
                    ins.then_inc(s_add, 1)

                def flush(s, whole, width, turned, signal):
                    first = dve.value_load(base_before[0:1, ds(s, 1)], min_val=0, max_val=NP - P)
                    dve.wait_ge(turned, s + 1)
                    v.tensor_tensor(whole[0:width, ds(first, P)], whole[0:width, ds(first, P)],
                                    ps_win[0:width, P:2 * P], ALU.add).then_inc(signal, 1)

                def one_hots(s, piece, again, used, made):
                    wide = WIDE1 if again else WIDE
                    if piece[0] == 0:
                        dve.wait_ge(s_bc[SRC], 16 * (s + 1 + again))
                    for j in piece:
                        dve.wait_ge(used, s * NB + j + 1)
                        v.tensor_scalar(one_of[:, hot_slot(j), 0:wide],
                                        ends_bc[SRC][:, ds(s % 2, 1), ES - wide:ES].rearrange("p a e -> p (a e)"),
                                        node_no[:, j:j + 1], None, ALU.is_equal).then_inc(made, 1)

                def ahead(s, g, again, used, made):
                    if windows and g in HOT_PIECES and not (isinstance(s, int) and g in HOT_EARLY):
                        one_hots(s + 1 if g in HOT_EARLY else s, HOT_PIECES[g], again, used, made)

                def next_idx(s, g, which, signal):
                    o = mine.index(g) + depth
                    if o < k_mine:
                        copy_idx(s, o, which, signal)
                    elif not (isinstance(s, int) and s == NS - 1):
                        copy_idx(s + 1, o - k_mine, which, signal)

                def split_window(s):
                    count = [0]

                    def after(ins):
                        count[0] += 1
                        ins.then_inc(s_split, 1)
                        dve.wait_ge(s_split, s * 3 + count[0])

                    dve.wait_ge(s_win_in, 16 * (s + 1))
                    at = ds(s % 2, 1)
                    split(win_rows[:, at, :].rearrange("p a f -> p (a f)"),
                          [win_parts[:, at, t, :].rearrange("p a f -> p (a f)") for t in range(PARTS)],
                          rest[:, :], after).then_inc(s_winp, 1)

                for o in range(depth):
                    copy_idx(0, o, sides, s_idx)
                window_T(0, 0, 0)
                prep(0, 0, 0)
                if windows:
                    v.memset(win_copy[:, :], 0.0).then_inc(s_winc, 1)
                    split_window(0)
                    for g in HOT_EARLY:
                        one_hots(0, HOT_PIECES[g], 0, s_xg, s_one)
                    dve.wait_ge(s_w, 16 * W_DMAS)
                    split(Wsrc[:, :], [Wsrc_parts[:, t, :] for t in range(PARTS)], rest[0:XW, :], link).then_inc(s_Wp, 1)

                def step(s, g):
                    n = s * GS + g
                    more = not (isinstance(s, int) and n == NG - 1)
                    if more:
                        window_T(n + 1, s + (g + 1) // GS, (g + 1) % GS)
                    if g in mine:
                        add(n, s, g)
                        next_idx(s, g, sides, s_idx)
                    if more:
                        prep(n + 1, s + (g + 1) // GS, (g + 1) % GS)
                    if windows and g == 0:
                        flush(s, hid_win_sum, HW, s_winn, s_win_free)
                    ahead(s, g, 0, s_xg, s_one)
                    if windows and g == 1 and not (isinstance(s, int) and s == NS - 1):
                        split_window(s + 1)

                with dve.Fori(0, NS - 1) as s:
                    for g in range(GS):
                        step(s, g)
                for g in range(GS):
                    step(NS - 1, g)
                if windows:
                    flush(NS, hid_win_sum, HW, s_winn, s_win_free)

                v.memset(uT[HID:HID + 1, :, :], 1.0)

                def add_tables(q):
                    j0, nj = CHUNKS[q]
                    table = [parts[:, t, j0:j0 + nj, :] for t in range(G)]
                    dve.wait_ge(s_parts[j0 >= HALVES[1][0]], 16 * G)
                    v.tensor_tensor(table[0], table[0], table[1], ALU.add)
                    link(v.tensor_tensor(table[2], table[2], table[3], ALU.add))
                    v.tensor_tensor(table[0], table[0], table[2], ALU.add).then_inc(s_psum, 1)

                for q in range(2):
                    add_tables(q)
                hid_cols = hid_win_sum[:, :].rearrange("f (p j) -> f j p", j=NB)
                for t in range(NC + 2):
                    if t < NC:
                        j0, nj = CHUNKS[t]
                        dve.wait_ge(s_sumT, t + 1)
                        v.tensor_tensor(hT[:, t % 2, 0:nj * P].rearrange("f (j p) -> f j p", j=nj),
                                        ps_pre[t % 2][0:HW, 0:nj * P].rearrange("f (j p) -> f j p", j=nj),
                                        hid_cols[:, j0:j0 + nj, :], ALU.add).then_inc(s_hT, 1)
                    if t + 2 < NC:
                        add_tables(t + 2)
                    if t >= 2:
                        j0, nj = CHUNKS[t - 2]
                        dve.wait_ge(s_second, t - 1)
                        v.tensor_tensor(y[:, j0:j0 + nj, :], xn[:, j0:j0 + nj, :],
                                        (ps_more, ps_win)[t % 2][:, 0:nj * F].rearrange("p (j f) -> p j f", j=nj),
                                        ALU.add).then_inc(s_y0, 1)

                def layer_norm(dest, source, turn):
                    y2 = squares

                    def across(small):
                        return small.rearrange("p (j a) -> p j a", a=1).to_broadcast([P, NB, F])
                    link(v.tensor_reduce(out=stat[:, 0, :], in_=source[:, :, :], axis=AX, op=ALU.add))
                    link(v.tensor_scalar(stat[:, 0, :], stat[:, 0, :], 1.0 / F, None, ALU.mult))
                    link(v.tensor_tensor(centred[:, :, :], source[:, :, :], across(stat[:, 0, :]), ALU.subtract))
                    link(v.tensor_tensor(y2[:, :, :], centred[:, :, :], centred[:, :, :], ALU.mult))
                    v.tensor_reduce(out=stat[:, 1, :], in_=y2[:, :, :], axis=AX, op=ALU.add).then_inc(s_sq, 1)
                    dve.wait_ge(s_sqd, turn)
                    link(v.reciprocal(stat[:, 3, :], stat[:, 2, :]))
                    return v.tensor_tensor(dest[:, :, :], centred[:, :, :], across(stat[:, 3, :]), ALU.mult)

                dve.wait_ge(s_y0, NC)
                v.memset(x1T(windows)[F:F + 1, :, :], 1.0)
                layer_norm(x1, y, 1).then_inc(s_x1, 1)
                if windows:
                    dve.wait_ge(s_x1, 1)
                    split_x(x1).then_inc(s_xp, 1)
                    v.memset(nei_win_sum, 0.0)

                def prep1(n, s, g):
                    count = [0]

                    def after(ins):
                        count[0] += 1
                        ins.then_inc(s_link1, 1)
                        dve.wait_ge(s_link1, n * 3 + count[0])

                    if not windows:
                        dve.wait_ge(s_mask1, n + 1)
                        dedup(DST, s, g, after).then_inc(s_prep1, 1)

                def copy_idx1(s, o):
                    v.tensor_copy(get_idx[SRC][o][:, :], col(SRC, s, o)).then_inc(s_idx1, 1)

                for o in range(R + 1 if windows else R):
                    copy_idx1(0, o)
                prep1(0, 0, 0)
                if windows:
                    v.memset(win_copy[:, :], 0.0).then_inc(s_win1c, 1)
                    for g in HOT_EARLY:
                        one_hots(0, HOT_PIECES[g], NS, s_xg1, s_one1)

                def step1(s, g):
                    n = s * GS + g
                    if g + 1 < GS:
                        prep1(n + 1, s, g + 1)
                    elif not (isinstance(s, int) and s == NS - 1):
                        prep1(n + 1, s + 1, 0)
                    if windows and 1 <= g <= R + 1:
                        for c in range(SHARED if g == R + 1 else G):
                            dve.wait_ge(s_got1[g - 1][c], 16 * (s + 1))
                        if not (isinstance(s, int) and s == NS - 1):
                            copy_idx1(s + 1, g - 1)
                    ahead(s, g, NS, s_xg1, s_one1)
                    if windows and g == 0:
                        flush(s, nei_win_sum, SW, s_win1n, s_win1_free)
                    if not windows:
                        dve.wait_ge(s_B1, R + n + 1)
                        next_idx(s, g, (SRC,), s_idx1)

                with dve.Fori(0, NS - 1) as s:
                    for g in range(GS):
                        step1(s, g)
                for g in range(GS):
                    step1(NS - 1, g)
                if windows:
                    flush(NS, nei_win_sum, SW, s_win1n, s_win1_free)
                else:
                    dve.wait_ge(s_parts1, 16 * G)
                    link(v.tensor_tensor(parts[:, 0, :, 0:SW], parts[:, 0, :, 0:SW], parts[:, 1, :, 0:SW], ALU.add))
                    link(v.tensor_tensor(parts[:, 2, :, 0:SW], parts[:, 2, :, 0:SW], parts[:, 3, :, 0:SW], ALU.add))
                    v.tensor_tensor(total[:, :, :], parts[:, 0, :, 0:SW], parts[:, 2, :, 0:SW], ALU.add).then_inc(s_total, 1)
                dve.wait_ge(s_x1Wc, 2)
                for h, (j0, nj) in enumerate(HALVES):
                    dve.wait_ge(s_nei, h + 1)
                    at = slice(j0, j0 + nj)
                    made = ps_pre[h][:, 0:nj * SW].rearrange("p (j f) -> p j f", j=nj)
                    link(v.tensor_scalar(stat[:, 0:1, at].rearrange("p a j -> p j a"), made[:, :, F:SW], 1.0, None, ALU.max))
                    link(v.reciprocal(stat[:, 1, at], stat[:, 0, at]))
                    link(v.tensor_tensor(y[:, at, :], made[:, :, 0:F],
                                         stat[:, 1, at].rearrange("p (j a) -> p j a", a=1).to_broadcast([P, nj, F]), ALU.mult))
                    link(v.tensor_tensor(y[:, at, :], y[:, at, :], x1W[:, at, :], ALU.add))
                    ins = v.scalar_tensor_tensor(y[:, at, :], y[:, at, :], 0.0, x1[:, at, :], ALU.max, ALU.add)
                link(ins)
                layer_norm(y, y, 2).then_inc(s_y, 1)

            with dve.If(fast == 1):
                program(True)
            with dve.Else():
                program(False)

        @block.tensor
        def _(pe):
            pe.wait_ge(s_const, 1)
            pe.wait_ge(s_x, 16)
            def x_T(q):
                j0, nj = CHUNKS[q]
                for j in range(nj):
                    last = nc.tensor.transpose((ps_more, ps_win)[q % 2][0:F, j * P:(j + 1) * P], xn[:, j0 + j, :], ident[:, :])
                last.then_inc(s_xT, 1)

            def turn_ends(side):
                pe.wait_ge(s_endsf, side + 1)
                for h in range(2):
                    if side:
                        pe.wait_ge(s_endsTc, h + 1)
                    for t in range(4):
                        first = (4 * h + t) * TC
                        last = nc.tensor.transpose(ps_dd[DST][h][0:TC, t * P:(t + 1) * P], ends_f[side][:, first:first + TC], ident[:, :])
                    last.then_inc(s_endsT, 1)

            x_T(0)
            pe.wait_ge(s_we, 16 * 5)
            for q, (j0, nj) in enumerate(CHUNKS):
                if q + 1 < NC:
                    x_T(q + 1)
                pe.wait_ge(s_xTc, q + 1)
                if q >= 2:
                    pe.wait_ge(s_rowsd, q - 1)
                    pe.wait_ge(s_rowsa, q - 1)
                for j in range(nj):
                    bank = ((ps_pre, ps_dd[SRC])[q % 2])[j // 2]
                    last = nc.tensor.matmul(bank[:, j % 2 * 4 * HID:(j % 2 + 1) * 4 * HID],
                                            xT[:, q % 2, j * P:(j + 1) * P], Wends[:, :], start=True, stop=True)
                last.then_inc(s_rows, 1)
                if q - ENDS_AT in (SRC, DST):
                    turn_ends(q - ENDS_AT)
            pe.wait_ge(s_reach, 1)
            nc.tensor.matmul(ps_win[0:1, 0:1], reach[:, 3:4], ones[:, 0:1], start=True, stop=True).then_inc(s_far, 1)
            pe.wait_ge(s_rowsd, NC)
            pe.wait_ge(s_rowsa, NC - 1)
            pe.wait_ge(s_flag, 1)
            fast = pe.value_load(flag[0:1, 0:1], min_val=0, max_val=1)

            def program(windows):
                sides = (SRC,) if windows else (SRC, DST)
                pe.sem_inc(s_B, R)
                pe.sem_inc(s_B1, R)
                pe.sem_inc(s_T, R)

                def ea_T(n, s, g):
                    loads = s * (GS // R) + g // R + 1
                    if isinstance(s, int) and s == NS - 1:
                        loads += g // R + 1
                    pe.wait_ge(s_ea[g % R], 16 * loads)
                    pe.nop(nofuse=True)
                    nc.tensor.transpose(
                        ps_dd[SRC][(g + 1) % 2][0:G * FE, EA_T:512],
                        ea_in[g % R][:, :, :].rearrange("p c f -> p (c f)"), ident[:, :]).then_inc(s_T, 1)

                mine, depth = plan(windows)

                def pre(n, s, g):
                    pe.wait_ge(s_Tc, n + 1)
                    if windows:
                        pe.wait_ge(s_winT, n + 1)
                    last = nc.tensor.matmul(ps_pre[g % 2][:, :], eaT[:, g % R, :],
                                            Cblk[:, :, :].rearrange("k c f -> k (c f)"), start=True, stop=not windows)
                    by_pe = g not in mine
                    if windows:
                        if g == 0:
                            pe.wait_ge(s_winp, s + 1)
                        for c in range(G):
                            for t in range(PARTS):
                                last = nc.tensor.matmul(ps_pre[g % 2][:, c * 2 * HID:(c + 1) * 2 * HID], in_winT[:, g % R, c, :],
                                                        win_parts[:, ds(s % 2, 1), t, :].rearrange("p a f -> p (a f)"),
                                                        start=False, stop=c == G - 1 and t == PARTS - 1 and not by_pe)
                    if by_pe:
                        pe.wait_ge(s_xgc, s * len(BY_PE) + BY_PE.index(g) + 1)
                        for c in range(G):
                            e0 = (BY_PE.index(g) * G + c) * P
                            for t in range(PARTS):
                                last = nc.tensor.matmul(ps_pre[g % 2][:, c * 2 * HID:(c + 1) * 2 * HID], xs[:, e0:e0 + P],
                                                        Wsrc_parts[:, t, :], start=False, stop=c == G - 1 and t == PARTS - 1)
                    last.then_inc(s_pre, 1)

                def ahead(s, g, made, used, product):
                    if windows and g in PIECES and not (isinstance(s, int) and s == NS - 1 and g in EARLY):
                        for j in PIECES[g]:
                            pe.wait_ge(made, (s + 1 if g in EARLY else s) * NB + j + 1)
                            product(j).then_inc(used, 1)

                def columns(j):
                    for k in range(len(BY_PE)):
                        last = nc.tensor.matmul(ps_src[k][0:XW, :], xparts[:, j, :], one_of[:, hot_slot(j), k * G * P:(k + 1) * G * P],
                                                start=j == 0, stop=j == NB - 1)
                    return last

                def rows(j, banks):
                    columns = WIDE1 // P
                    for c in range(columns):
                        last = nc.tensor.matmul(banks[c // G][:, c % G * XW:(c % G + 1) * XW], one_of[:, hot_slot(j), c * P:(c + 1) * P],
                                                xparts[:, j, :], start=j == 0 and c % G == 0,
                                                stop=j == NB - 1 and (c % G == G - 1 or c == columns - 1))
                    return last

                def use(n, s, g):
                    pe.wait_ge(s_hid, n + 1)
                    if g + R < GS:
                        ea_T(n + R, s, g + R)
                    elif not (isinstance(s, int) and s == NS - 1):
                        ea_T(n + R, s + 1, g + R - GS)
                    pe.wait_ge(s_mask, n + 1)
                    for side in sides:
                        for c in range(G):
                            h0 = HW * (1 - side)
                            last = nc.tensor.matmul(ps_dd[side][g % 2][:, c * HW:(c + 1) * HW], same[side][:, g % R, c, :],
                                                    hid[:, g % 2, c, h0:h0 + HW], start=True, stop=True)
                    if windows:
                        if g == 0:
                            pe.wait_ge(s_win_free, s + 1)
                        for c in range(G):
                            last = nc.tensor.matmul(ps_win[:, 0:HW], in_win[:, g % R, c, :], hid[:, g % 2, c, 0:HW],
                                                    start=g == 0 and c == 0, stop=g == GS - 1 and c == G - 1)
                    last.then_inc(s_B, 1)

                def turn(s, width, copied, turned):
                    pe.wait_ge(copied, s + 1)
                    pe.nop(nofuse=True)
                    nc.tensor.transpose(ps_win[0:width, P:2 * P], win_copy[:, 0:width], ident[:, :]).then_inc(turned, 1)

                pe.wait_ge(s_w, 16 * W_DMAS)
                if windows:
                    pe.wait_ge(s_xp, 1)
                    pe.sem_inc(s_xg, HOT)
                    pe.sem_inc(s_xg1, HOT)
                ea_T(0, 0, 0)
                pre(0, 0, 0)
                ea_T(1, 0, 1)
                pe.wait_ge(s_Tc, 1)
                ea_T(2, 0, 2)
                for g in EARLY:
                    ahead(-1, g, s_one, s_xg, columns)
                if windows:
                    pe.wait_ge(s_Wp, 1)

                def step(s, g):
                    n = s * GS + g
                    end = isinstance(s, int) and s == NS - 1
                    if windows and g == 0:
                        turn(s, HW, s_winc, s_winn)
                    if g + 1 < GS:
                        pre(n + 1, s, g + 1)
                    elif not end:
                        pre(n + 1, s + 1, 0)
                    use(n, s, g)
                    if windows and PIECES.get(g, (1,))[0] == 0:
                        pe.wait_ge(s_xgc, (s + 1) * len(BY_PE))
                    ahead(s, g, s_one, s_xg, columns)

                with pe.Fori(0, NS - 2) as s:
                    for g in range(GS):
                        step(s, g)
                for s in (NS - 2, NS - 1):
                    for g in range(GS):
                        step(s, g)

                if windows:
                    turn(NS, HW, s_winc, s_winn)

                nc.tensor.transpose(ps_more[0:HID, 0:HW], Wf2b[:, :], ident[0:HW, 0:HW]).then_inc(s_W2T, 1)
                pe.wait_ge(s_W2Tc, 1)
                nc.tensor.matmul(ps_more[0:HW, 0:HID], W2T[:, :], Wn1s[:, :], start=True, stop=True).then_inc(s_W21, 1)
                pe.wait_ge(s_W21c, 1)
                for t in range(NC + 2):
                    if t < NC:
                        pe.wait_ge(s_psum, t + 1)
                        j0, nj = CHUNKS[t]
                        for j in range(nj):
                            last = nc.tensor.transpose(ps_pre[t % 2][0:HW, j * P:(j + 1) * P], parts[:, 0, j0 + j, :], ident[:, :])
                        last.then_inc(s_sumT, 1)
                    if 1 <= t <= NC:
                        q = t - 1
                        w = CHUNKS[q][1] * P
                        pe.wait_ge(s_hT, q + 1)
                        nc.tensor.matmul(ps_dd[1][q % 2][0:HID, 0:w], W21[:, :], hT[:, q % 2, 0:w], start=True, stop=True).then_inc(s_u, 1)
                    if t >= 2:
                        q = t - 2
                        pe.wait_ge(s_uT, q + 1)
                        if q >= 2:
                            pe.wait_ge(s_y0, q - 1)
                        for j in range(CHUNKS[q][1]):
                            last = nc.tensor.matmul((ps_more, ps_win)[q % 2][:, j * F:(j + 1) * F], uT[:, q % 2, j * P:(j + 1) * P],
                                                    Wn2b[:, :], start=True, stop=True)
                        last.then_inc(s_second, 1)

                pe.wait_ge(s_x1, 1)

                def x1_T(q):
                    j0, nj = CHUNKS[q]
                    for j in range(nj):
                        last = nc.tensor.transpose(ps_pre[q % 2][0:F, j * P:(j + 1) * P], x1[:, j0 + j, :], ident[:, :])
                    last.then_inc(s_x1T, 1)

                x1_T(0)
                for q, (j0, nj) in enumerate(CHUNKS):
                    if q + 1 < NC:
                        x1_T(q + 1)
                    pe.wait_ge(s_x1Tc, q + 1)
                    for j in range(j0, j0 + nj):
                        h = int(j >= HALVES[1][0])
                        at = (j - HALVES[h][0]) * F
                        last = nc.tensor.matmul(ps_dd[SRC][h][:, at:at + F], x1T(windows)[:, q % 2, (j - j0) * P:(j - j0 + 1) * P],
                                                Wself[:, :], start=True, stop=True)
                    if j0 + nj in (HALVES[1][0], NB):
                        last.then_inc(s_x1W, 1)

                def use1(n, s, g):
                    pe.wait_ge(s_mask1, n + 1)
                    if windows and g == 0:
                        pe.wait_ge(s_win1_free, s + 1)
                    by_pool = 0 if windows and g in BY_PE else G
                    if windows and g == BY_PE[0]:
                        by_pool = SHARED
                    if windows:
                        slot, fills = g, s + 1
                    else:
                        slot, fills = g % R, s * (GS // R) + g // R + 1
                    for c in range(by_pool):
                        pe.wait_ge(s_got1[slot][c], 16 * fills)
                    for c in range(by_pool):
                        if windows:
                            last = nc.tensor.matmul(ps_win[:, 0:SW], in_win[:, g % R, c, :], got1[:, slot, c, :],
                                                    start=g == 0 and c == 0, stop=False)
                        else:
                            last = nc.tensor.matmul(ps_dd[DST][g % 2][:, c * SW:(c + 1) * SW], same[DST][:, g % R, c, :],
                                                    got1[:, slot, c, :], start=True, stop=True)
                    if by_pool < G:
                        k = BY_PE.index(g)
                        pe.wait_ge(s_xg1c, s * len(BY_PE) + k + 1)
                        for c in range(by_pool, G):
                            for t in range(PARTS):
                                width = SW if t == PARTS - 1 else F
                                last = nc.tensor.matmul(ps_win[:, 0:width], in_win_b[:, k, c, :], xg[:, k * G + c - SHARED, t * F:t * F + width],
                                                        start=False, stop=g == GS - 1 and c == G - 1 and t == PARTS - 1)
                    last.then_inc(s_B1, 1)

                if windows:
                    pe.wait_ge(s_xp, 2)
                pe.wait_ge(s_y0, NC)
                pe.wait_ge(s_x1Wc, 2)
                if windows:
                    for g in EARLY:
                        ahead(-1, g, s_one1, s_xg1, lambda j: rows(j, ps_src1[0]))

                def step1(s, parity, g):
                    if not windows:
                        pe.wait_ge(s_sums1, s * GS + g + 1)
                    if windows and g == 0:
                        turn(s, SW, s_win1c, s_win1n)
                    banks = ps_src1[(parity + (g in EARLY)) % 2]
                    ahead(s, g, s_one1, s_xg1, lambda j: rows(j, banks))
                    use1(s * GS + g, s, g)

                with pe.Fori(0, NS // 2 - 1) as pair:
                    for parity in range(2):
                        for g in range(GS):
                            step1(pair * 2 + parity, parity, g)
                for s in (NS - 2, NS - 1):
                    for g in range(GS):
                        step1(s, s % 2, g)
                def products(j0, nj, columns):
                    for j in range(j0, j0 + nj):
                        h = int(j >= HALVES[1][0])
                        at = (j - HALVES[h][0]) * SW
                        last = nc.tensor.matmul(ps_pre[h][:, at:at + SW], columns(j), Wnei[:, :], start=True, stop=True)
                    if j0 + nj in (HALVES[1][0], NB):
                        last.then_inc(s_nei, 1)

                if windows:
                    turn(NS, SW, s_win1c, s_win1n)
                    pe.wait_ge(s_win1_free, NS + 1)
                    win_cols = nei_win_sum.rearrange("f (p j) -> f j p", j=NB)
                    for j0, nj in HALVES:
                        products(j0, nj, lambda j: win_cols[:, j, :])
                else:
                    pe.wait_ge(s_total, 1)

                    def total_T(q):
                        j0, nj = CHUNKS[q]
                        for j in range(nj):
                            last = nc.tensor.transpose(ps_dd[SRC][q % 2][0:SW, j * P:(j + 1) * P], total[:, j0 + j, :], ident[:, :])
                        last.then_inc(s_totalT, 1)

                    total_T(0)
                    for q, (j0, nj) in enumerate(CHUNKS):
                        if q + 1 < NC:
                            total_T(q + 1)
                        pe.wait_ge(s_totalTc, q + 1)
                        products(j0, nj, lambda j: nT[:, q % 2, (j - j0) * P:(j - j0 + 1) * P])

            with pe.If(fast == 1):
                program(True)
            with pe.Else():
                program(False)


_INS = ['x', 'src', 'dst', 'edge_attr_16', 'L0_gnn_Wf1', 'L0_gnn_bf1', 'L0_gnn_Wf2', 'L0_gnn_bf2', 'L0_gnn_Wn1',
        'L0_gnn_bn1', 'L0_gnn_Wn2', 'L0_gnn_bn2', 'L1_gnn_W', 'L1_gnn_b']
_OUTS = [((N, F), 'float32')]


def kernel(**inputs):
    import numpy as _np
    import concourse.bacc as _bacc
    from concourse import mybir as _mybir
    from concourse.bass_utils import run_bass_kernel_spmd as _run

    nc = _bacc.Bacc("TRN2", target_bir_lowering=False, num_devices=1)
    arrays, args = {}, []
    for name in _INS:
        a = _np.ascontiguousarray(inputs[name])
        arrays[f"in_{name}_dram"] = a
        args.append(nc.dram_tensor(f"in_{name}_dram", a.shape, _mybir.dt.from_np(a.dtype), kind="ExternalInput").ap())
    for i, (shape, dtype) in enumerate(_OUTS):
        dt = _mybir.dt.from_np(_np.dtype(dtype))
        args.append(nc.dram_tensor(f"out_{i}_dram", shape, dt, kind="ExternalOutput").ap())
    build(nc, *args)
    r = _run(nc, [arrays], core_ids=[0])
    got = tuple(r.results[0][f"out_{i}_dram"] for i in range(len(_OUTS)))
    return got[0]
```
